# Optimizing a Trainium2 kernel written in Bass

```python
import numpy as np
import jax
import jax.numpy as jnp

def _softmax(x, axis=-1):
    return jax.nn.softmax(x, axis=axis)

def _gelu(x):
    return jax.nn.gelu(x, approximate=True)

def _silu(x):
    return jax.nn.silu(x)

def _sigmoid(x):
    return jax.nn.sigmoid(x)

def _layernorm(x, axis=-1, eps=1e-05):
    m = jnp.mean(x, axis=axis, keepdims=True)
    v = jnp.var(x, axis=axis, keepdims=True)
    return (x - m) / jnp.sqrt(v + eps)

def _scatter_add(tgt, idx, src, axis=0):
    return tgt.at[idx].add(src)

def _segment_sum(src, seg, n):
    return jax.ops.segment_sum(src, seg, n)
kernel_name = 'mk_prb_d1_jaxref_r4_065ae3'

def setup_inputs(seed: int=0):
    np.random.seed(seed)
    _w = jnp.asarray

    def _L0_attn_setup():
        import jax, jax.numpy as jnp
        import numpy as np
        N_HEAD = 16
        MASK_SCALE = 10000.0

        def _shaped_attention(x, W_attn, alpha, beta, gamma):
            B, T, C = x.shape
            H = N_HEAD
            hd = C // H
            qk = jnp.einsum('btc,oc->bto', x, W_attn)
            q, k = jnp.split(qk, 2, axis=-1)
            q = q.reshape(B, T, H, hd).transpose(0, 2, 1, 3)
            k = k.reshape(B, T, H, hd).transpose(0, 2, 1, 3)
            v = x.reshape(B, T, H, hd).transpose(0, 2, 1, 3)
            scores = jnp.einsum('bhqd,bhkd->bhqk', q, k) * hd ** (-0.5)
            tril = jnp.tril(jnp.ones((T, T), dtype=bool))
            scores = jnp.where(tril, scores, -jnp.inf)
            att = jax.nn.softmax(scores, axis=-1)
            Id = jax.nn.softmax(jnp.eye(T, dtype=jnp.float32) * MASK_SCALE, axis=-1)
            MC = jax.nn.softmax(tril.astype(jnp.float32) * MASK_SCALE, axis=-1)
            shaped = beta * att + alpha * Id[None, None] - gamma * MC[None, None]
            y = jnp.einsum('bhqk,bhkd->bhqd', shaped, v)
            return y.transpose(0, 2, 1, 3).reshape(B, T, C)
        key = jax.random.key(seed)
        k1, k2 = jax.random.split(key)
        B, T, C = (2, 512, 256)
        x = jax.random.normal(k1, (B, T, C), dtype=jnp.float32)
        W_attn = jax.random.normal(k2, (2 * C, C), dtype=jnp.float32) * 0.02
        alpha = jnp.array(1.0, dtype=jnp.float32)
        beta = jnp.array(0.1, dtype=jnp.float32)
        gamma = jnp.array(0.1, dtype=jnp.float32)
        return {'x': x, 'W_attn': W_attn, 'alpha': alpha, 'beta': beta, 'gamma': gamma}
    _L0_attn_in = _L0_attn_setup()

    def _L0_ffn_setup():
        import jax, jax.numpy as jnp
        import numpy as np
        B, N, C, H, REG = (1, 2309, 256, 16, 5)
        D = C // H
        key = jax.random.key(seed)
        k0, k1, k2, k3 = jax.random.split(key, 4)
        x = jax.random.normal(k0, (B, N, C), dtype=jnp.float32)
        g_info = jax.random.normal(k1, (12, 2, C), dtype=jnp.float32)
        W_qkv = jax.random.normal(k2, (C, 3 * C), dtype=jnp.float32) * 0.02
        W_proj = jax.random.normal(k3, (C, C), dtype=jnp.float32) * 0.02
        b_proj = jnp.zeros((C,), dtype=jnp.float32)
        return {'x': x, 'g_info': g_info, 'W_qkv': W_qkv, 'W_proj': W_proj, 'b_proj': b_proj}
    _L0_ffn_in = _L0_ffn_setup()
    _d = {'L0_attn_x': _L0_attn_in['x'], 'L0_attn_W_attn': _L0_attn_in['W_attn'], 'L0_attn_alpha': _L0_attn_in['alpha'], 'L0_attn_beta': _L0_attn_in['beta'], 'L0_attn_gamma': _L0_attn_in['gamma'], 'L0_ffn_g_info': _L0_ffn_in['g_info'], 'L0_ffn_W_qkv': _L0_ffn_in['W_qkv'], 'L0_ffn_W_proj': _L0_ffn_in['W_proj'], 'L0_ffn_b_proj': _L0_ffn_in['b_proj']}
    _x0 = _d['L0_attn_x']
    _d['L0_attn_x'] = jax.random.normal(jax.random.fold_in(jax.random.key(seed), 1), (4, 2048, 256), dtype=_x0.dtype)
    del _x0
    return _d

def reference(L0_attn_x, L0_attn_W_attn, L0_attn_alpha, L0_attn_beta, L0_attn_gamma, L0_ffn_g_info, L0_ffn_W_qkv, L0_ffn_W_proj, L0_ffn_b_proj):

    def _L0_attn_ref(x, W_attn, alpha, beta, gamma):
        import jax, jax.numpy as jnp
        import numpy as np
        N_HEAD = 16
        MASK_SCALE = 10000.0

        def _shaped_attention(x, W_attn, alpha, beta, gamma):
            B, T, C = x.shape
            H = N_HEAD
            hd = C // H
            qk = jnp.einsum('btc,oc->bto', x, W_attn)
            q, k = jnp.split(qk, 2, axis=-1)
            q = q.reshape(B, T, H, hd).transpose(0, 2, 1, 3)
            k = k.reshape(B, T, H, hd).transpose(0, 2, 1, 3)
            v = x.reshape(B, T, H, hd).transpose(0, 2, 1, 3)
            scores = jnp.einsum('bhqd,bhkd->bhqk', q, k) * hd ** (-0.5)
            tril = jnp.tril(jnp.ones((T, T), dtype=bool))
            scores = jnp.where(tril, scores, -jnp.inf)
            att = jax.nn.softmax(scores, axis=-1)
            Id = jax.nn.softmax(jnp.eye(T, dtype=jnp.float32) * MASK_SCALE, axis=-1)
            MC = jax.nn.softmax(tril.astype(jnp.float32) * MASK_SCALE, axis=-1)
            shaped = beta * att + alpha * Id[None, None] - gamma * MC[None, None]
            y = jnp.einsum('bhqk,bhkd->bhqd', shaped, v)
            return y.transpose(0, 2, 1, 3).reshape(B, T, C)
        return _shaped_attention(x, W_attn, alpha, beta, gamma)

    def _L0_ffn_ref(x, g_info, W_qkv, W_proj, b_proj):
        import jax, jax.numpy as jnp
        import numpy as np
        B, N, C, H, REG = (1, 2309, 256, 16, 5)
        D = C // H
        Bx, Nx, Cx = x.shape
        scale = D ** (-0.5)
        qkv = (x @ W_qkv).reshape(Bx, Nx, 3, H, D)
        q, k, v = (qkv[:, :, 0], qkv[:, :, 1], qkv[:, :, 2])
        g_layer = g_info[0].reshape(-1, H, D)
        q_g = g_layer[0]
        q_pure = q[:, REG:]
        q_n = q_pure / jnp.linalg.norm(q_pure, axis=-1, keepdims=True)
        qg_n = q_g / jnp.linalg.norm(q_g, axis=-1, keepdims=True)
        sim = (qg_n[None, None] * q_n).sum(-1).mean(-1)
        sim = (sim - sim.min()) / (sim.max() - sim.min())
        pos = sim > 0.9
        logits = jnp.einsum('bqhd,bkhd->bhqk', q * scale, k)

        def masked_attn(tok_mask):
            key_mask = jnp.concatenate([jnp.ones((Bx, REG), bool), tok_mask], axis=1)
            l = jnp.where(key_mask[:, None, None, :], logits, -jnp.inf)
            a = jax.nn.softmax(l, axis=-1)
            return jnp.einsum('bhqk,bkhd->bqhd', a, v)
        x_pos = masked_attn(pos)
        x_neg = masked_attn(~pos)
        reg_out = (x_pos[:, :REG] + x_neg[:, :REG]) * 0.5
        tok_out = jnp.where(pos[:, :, None, None], x_pos[:, REG:], x_neg[:, REG:])
        out = jnp.concatenate([reg_out, tok_out], axis=1).reshape(Bx, Nx, Cx)
        return out @ W_proj + b_proj
    x = L0_attn_x
    xn = _layernorm(x, axis=-1)
    x = x + _L0_attn_ref(xn, L0_attn_W_attn, L0_attn_alpha, L0_attn_beta, L0_attn_gamma) + _L0_ffn_ref(xn, L0_ffn_g_info, L0_ffn_W_qkv, L0_ffn_W_proj, L0_ffn_b_proj)
    return x

_drawn_inputs = setup_inputs


def setup_inputs(seed=0):
    import zlib

    import numpy as np

    out = dict(_drawn_inputs(seed))
    spreads = {'L0_ffn_b_proj': (0.0, 0.411)}
    factors = {'L0_attn_W_attn': 29.972, 'L0_ffn_g_info': 8.0, 'L0_ffn_W_qkv': 8.0, 'L0_ffn_W_proj': 8.0}
    for name, (base, spread) in spreads.items():
        noise = np.random.default_rng([zlib.crc32(name.encode()), seed]).standard_normal(out[name].shape)
        drawn = base * np.exp(spread * noise) if base else spread * noise
        out[name] = jnp.asarray(drawn.astype(out[name].dtype))
    for name, factor in factors.items():
        out[name] = (out[name] * factor).astype(out[name].dtype)
    return out
```

```python
from contextlib import ExitStack

import numpy as np

import concourse.bass as bass
from concourse import mybir

F32 = mybir.dt.float32
BF16 = mybir.dt.bfloat16
ALU = mybir.AluOpType
ACT = mybir.ActivationFunctionType
AX = mybir.AxisListType

P = 128
B, T, C = 4, 2048, 256
H = 16
D = C // H
REG = 5
HG = 4
GROUPS = B * H // HG
GPB = H // HG
QB = 512
QBLOCKS = T // QB
KTILES = T // P
CHUNKS = B * QBLOCKS
KC = C // P
VW = D + 1
SPLIT_ROWS = 6 * D
Q_PART = (0, 0, 1, 0, 1, 2)
K_PART = (0, 1, 0, 2, 1, 0)
SCALE = float(D) ** -0.5
MASKED = -(2.0 ** 40)
EPS = 1e-5
LAG = 2
PRING = 4
REG_UNIT = -1


def wait_apart(engine, sem, value, passed):
    engine.wait_ge(sem, value)
    engine.sem_inc(passed, 1)


def attend_plan(causal):
    units, steps, last_step = [], [], {}
    for half in range(2):
        for i in list(range(QBLOCKS)) + ([] if causal else [REG_UNIT]):
            units.append((half, i))
            n = 1 if i == REG_UNIT else (4 * (i + 1) if causal else KTILES)
            for j in range(n):
                steps.append((len(units) - 1, half, i, j))
            last_step[len(steps) - 1] = len(units) - 1
    return units, steps, last_step


def max_blocks(causal, i):
    return [(h, t, kb) for h in range(HG) for t in range(4) for kb in range((i + 1) if causal else QBLOCKS)]


def max_share(causal, units, steps, last_step, pos):
    u, half, i, j = steps[pos]
    if i == REG_UNIT:
        return None
    ahead_half, ahead_i = (half, i + 2) if i < 2 else (1 - half, i - 2)
    blocks = max_blocks(causal, ahead_i)
    n = 4 * (i + 1) if causal else KTILES
    a, b = (len(blocks) * j) // n, (len(blocks) * (j + 1)) // n
    return ahead_half, ahead_i, blocks[a:b]


def attend(nc, sems, causal, parts, values, masks, reg_rows, result, reg_result, const):
    tag = "causal" if causal else "class"
    units, steps, last_step = attend_plan(causal)
    NSTEP, NUNIT = len(steps), len(units)
    MAIN = sum(i != REG_UNIT for _, i in units)
    MROW = SPLIT_ROWS if causal else SPLIT_ROWS + 2
    KMAX, KEXP = MROW, MROW + 2
    NREG = NUNIT - MAIN
    LEAD_BLOCKS = len(max_blocks(causal, 0)) + len(max_blocks(causal, 1))
    LEAD = LEAD_BLOCKS + 2
    BODY = sum(len(max_blocks(causal, i)) for _, i in units if i != REG_UNIT) + MAIN + NUNIT + NREG * (QBLOCKS + 1)
    LOADS = 6 * 2 + 1 + (0 if causal else 8 + 6 + 1)
    M_STEPS = 2
    LEAD_STEPS = 2 * M_STEPS
    BODY_STEPS = MAIN * M_STEPS + NREG * M_STEPS + NUNIT
    NBODY = GROUPS // 2
    ROWS_DMA = 16 * 2 * HG

    with ExitStack() as ctx:
        def sb(name, shape, dt):
            return ctx.enter_context(nc.sbuf_tensor(f"{tag}_{name}", shape, dt))

        def ps(name, shape, dt):
            return ctx.enter_context(nc.psum_tensor(f"{tag}_{name}", shape, dt))

        def sem(name):
            return sems.enter_context(nc.semaphore(f"{tag}_{name}"))

        kt = [sb(f"kt{p}", [SPLIT_ROWS + 4, HG, T], BF16) for p in range(2)]
        qt = [sb(f"qt{p}", [SPLIT_ROWS + 4, HG, T], BF16) for p in range(2)]
        qr = [sb(f"qr{p}", [SPLIT_ROWS + 4, HG, 32], BF16) for p in range(2)]
        vt = [sb(f"vt{p}", [P, KTILES, HG, VW], F32) for p in range(2)]
        prob = sb("prob", [P, PRING, HG, QB], F32)
        o_sb = sb("o_sb", [P, 2, QB], F32)
        y_sb = sb("y_sb", [P, 2, 4 * HG, D], F32)
        part_max = sb("part_max", [P, 16, QBLOCKS], F32)
        minus_max = sb("minus_max", [P, 16], F32)
        high_max = sb("high_max", [P, 16], BF16)
        packed = sb("packed", [P, 2, 16], F32)
        turned = sb("turned", [32, P], BF16)
        reg_part = sb("reg_part", [P, QBLOCKS], F32)
        reg_minus = sb("reg_minus", [P, 1], F32)
        reg_high = sb("reg_high", [P, 1], BF16)
        reg_packed = sb("reg_packed", [P, 2], F32)
        reg_turned = sb("reg_turned", [2, P], BF16)
        inv = sb("inv", [P, 2, 16], F32)
        small = [ps(f"small{s}", [P, QB], F32) for s in range(3)]
        score = ps("score", [P, 2, 2, QB], F32)
        o_ps = ps("o_ps", [P, QB], F32)

        loaded = [sem(f"loaded{p}") for p in range(2)]
        ones_set = sem("ones_set")
        cleared = sem("cleared")
        item_made = sem("item_made")
        item_used = sem("item_used")
        step_done = sem("step_done")
        max_packed = sem("max_packed")
        reg_max_packed = sem("reg_max_packed")
        rows_in = sem("rows_in")
        reg_rows_in = sem("reg_rows_in")
        score_made = sem("score_made")
        exp_done = sem("exp_done")
        pv_done = sem("pv_done")
        o_copied = sem("o_copied")
        y_stored = [sem(f"y_stored{s}") for s in range(2)]

        passed_sp = sem("passed_sp")
        block = ctx.enter_context(nc.Block())

        def reg_lead(pos):
            return pos < NSTEP and not causal and steps[pos][2] == 0 and steps[pos][3] == 1

        @block.sync
        def _(sp):
            def load(n, par):
                for r in range(6):
                    rows = bass.ds(n * HG * D, HG * D)
                    for dst, part in ((kt[par], parts[1][K_PART[r]]), (qt[par], parts[0][Q_PART[r]])):
                        sp.dma_start(dst[r * D:(r + 1) * D, :, :],
                                     part[rows, :].rearrange("(h d) t -> d h t", d=D)).then_inc(loaded[par], 16)
                    if not causal:
                        sp.dma_start(qr[par][r * D:(r + 1) * D, :, :],
                                     parts[0][Q_PART[r]][rows, 0:32].rearrange("(h d) t -> d h t", d=D))\
                          .then_inc(loaded[par], 16)
                sp.dma_start(vt[par][:, :, :, :].rearrange("p k h e -> p (k h e)"),
                             values[bass.ds(n, 1)].rearrange("o p x -> (o p) x")).then_inc(loaded[par], 16)
                if not causal:
                    for h in range(HG):
                        b = n // 4
                        sp.dma_start(kt[par][SPLIT_ROWS:SPLIT_ROWS + 2, h, :],
                                     masks[0:2, bass.ds(b, 1), :].rearrange("k o t -> k (o t)"))\
                          .then_inc(loaded[par], 16)
                        sp.dma_start(qt[par][SPLIT_ROWS:SPLIT_ROWS + 2, h, :],
                                     masks[2:4, bass.ds(b, 1), :].rearrange("k o t -> k (o t)"))\
                          .then_inc(loaded[par], 16)
                    sp.dma_start(qr[par][SPLIT_ROWS:SPLIT_ROWS + 2, :, :].rearrange("r h q -> r (h q)"),
                                 reg_rows).then_inc(loaded[par], 16)

            def store_rows(par, i, used):
                sp.wait_ge(item_used, used)
                for r in range(2):
                    for h in range(HG):
                        sp.dma_start(qt[par][MROW + r:MROW + r + 1, h, i * QB:(i + 1) * QB],
                                     turned[16 * r + 4 * h:16 * r + 4 * h + 4, :]).then_inc(rows_in, 16)

            sp.wait_ge(ones_set, 2)
            load(0, 0)
            k = 0
            for i in range(2):
                k += len(max_blocks(causal, i)) + 1
                store_rows(0, i, k)
            with sp.Fori(0, NBODY) as it:
                k = 0
                for pos in range(NSTEP + LAG + 2):
                    if pos < NSTEP:
                        u, half, i, j = steps[pos]
                        if i == 1 and j == 0:
                            wait_apart(sp, pv_done, it * NSTEP + pos, passed_sp)
                            load((it * 2 + (half + 1)) % GROUPS, 1 - half)
                        if i != REG_UNIT:
                            k += len(max_share(causal, units, steps, last_step, pos)[2])
                        if reg_lead(pos):
                            k += QBLOCKS + 1
                            wait_apart(sp, item_used, it * BODY + (LEAD + k), passed_sp)
                            sp.dma_start(qr[half][SPLIT_ROWS + 2:SPLIT_ROWS + 4, :, :]
                                         .rearrange("r h q -> r (h q)"),
                                         reg_turned[:, :]).then_inc(reg_rows_in, 16)
                    if pos - LAG - 1 in last_step:
                        u = last_step[pos - LAG - 1]
                        half, i = units[u]
                        k += 1
                        wait_apart(sp, item_used, it * BODY + (LEAD + k), passed_sp)
                        n = it * 2 + half
                        if i == REG_UNIT:
                            sp.dma_start(reg_result[bass.ds(n, 1)].rearrange("o r x -> (o r) x"),
                                         y_sb[0:8, u % 2, 0:HG, :].rearrange("p a d -> p (a d)"))\
                              .then_inc(y_stored[u % 2], 16)
                        else:
                            sp.dma_start(result[bass.ds(n, 1), i].rearrange("o p x -> (o p) x"),
                                         y_sb[:, u % 2, :, :].rearrange("p a d -> p (a d)")).then_inc(y_stored[u % 2], 16)
                    if pos in last_step and units[last_step[pos]][1] != REG_UNIT:
                        half, i = units[last_step[pos]]
                        k += 1
                        ahead_half, ahead_i = (half, i + 2) if i < 2 else (1 - half, i - 2)
                        store_rows(ahead_half, ahead_i, it * BODY + (LEAD + k))
            for s in range(2):
                sp.wait_ge(y_stored[s], 16 * (1 + NBODY * NUNIT // 2))
            sp.wait_ge(rows_in, ROWS_DMA * (2 + NBODY * MAIN))

        @block.gpsimd
        def _(pool):
            for p in range(2):
                nc.gpsimd.memset(kt[p][SPLIT_ROWS:SPLIT_ROWS + 4, :, :], 1.0).then_inc(ones_set, 1)

        @block.tensor
        def _(pe):
            ident = const["ident"]

            def slot(k):
                return small[(k - LEAD) % 3]

            def max_item(par, i, h, t, kb, k, free):
                if free is not None:
                    pe.wait_ge(item_used, free)
                diag = causal and kb == i
                w = P * (t + 1) if diag else QB
                lhs = qt[par][0:KMAX, h, i * QB + t * P:i * QB + (t + 1) * P]
                mm = nc.tensor.matmul(slot(k)[:, 0:w], lhs, kt[par][0:KMAX, h, kb * QB:kb * QB + w],
                                      start=True, stop=not diag)
                if diag:
                    mm = nc.tensor.matmul(slot(k)[:, w - P:w], const["ident_bf"][:, :], const["mask_max"][:, :],
                                          start=False, stop=True)
                mm.then_inc(item_made, 1)

            def turn_max(k, packs, free):
                pe.wait_ge(max_packed, packs)
                pe.wait_ge(item_used, free)
                nc.tensor.transpose(slot(k)[0:32, 0:P], packed[:, :, :].rearrange("p r a -> p (r a)"),
                                    ident[:, :]).then_inc(item_made, 1)

            pe.wait_ge(ones_set, 2)
            pe.wait_ge(cleared, 1)
            pe.wait_ge(loaded[0], 16 * LOADS)
            k = 0
            for i in range(2):
                for h, t, kb in max_blocks(causal, i):
                    max_item(0, i, h, t, kb, k, k - 2 if k >= 3 else None)
                    k += 1
                turn_max(k, i + 1, k - 2)
                k += 1
            with pe.Fori(0, NBODY) as it:
                k, e, main = 0, 0, 0
                for pos in range(NSTEP + LAG + 2):
                    if pos < NSTEP:
                        u, half, i, j = steps[pos]
                        if i == REG_UNIT:
                            pe.wait_ge(reg_rows_in, it * 32 + 16 * (half + 1))
                            for two in range(2):
                                pe.wait_ge(exp_done, it * (2 * NSTEP) + (e - 1))
                                for j8 in range(8):
                                    for h in range(HG):
                                        jj = 8 * two + j8
                                        mm = nc.tensor.matmul(
                                            score[:, e % 2, 0, (j8 * HG + h) * 8:(j8 * HG + h) * 8 + 8],
                                            kt[half][0:KEXP, h, jj * P:(jj + 1) * P], qr[half][0:KEXP, h, 0:8],
                                            start=True, stop=True)
                                mm.then_inc(score_made, 1)
                                e += 1
                        else:
                            ahead_half, ahead_i, blocks = max_share(causal, units, steps, last_step, pos)
                            if j == 0:
                                pe.wait_ge(rows_in, it * (ROWS_DMA * MAIN) + ROWS_DMA * (main + 1))
                                main += 1
                                if ahead_i == 0:
                                    pe.wait_ge(loaded[ahead_half], it * (16 * LOADS) + 16 * LOADS * (1 + half))
                            lo = P * (j - 4 * i) if causal and j >= 4 * i else 0
                            for two in range(2):
                                if e >= 2:
                                    pe.wait_ge(exp_done, it * (2 * NSTEP) + (e - 1))
                                for hh in range(2):
                                    h = 2 * two + hh
                                    diag = causal and j >= 4 * i
                                    mm = nc.tensor.matmul(score[:, e % 2, hh, lo:QB],
                                                          kt[half][0:KEXP, h, j * P:(j + 1) * P],
                                                          qt[half][0:KEXP, h, i * QB + lo:(i + 1) * QB],
                                                          start=True, stop=not diag)
                                    if diag:
                                        mm = nc.tensor.matmul(score[:, e % 2, hh, lo:lo + P],
                                                              const["ident_bf"][:, :], const["mask_exp"][:, :],
                                                              start=False, stop=True)
                                mm.then_inc(score_made, 1)
                                e += 1
                                cut = (len(blocks) + 1) // 2
                                for h, t, kb in (blocks[:cut] if two == 0 else blocks[cut:]):
                                    max_item(ahead_half, ahead_i, h, t, kb, LEAD + k, it * BODY + (LEAD + k - 2))
                                    k += 1
                        if reg_lead(pos):
                            for kb in range(QBLOCKS):
                                pe.wait_ge(item_used, it * BODY + (LEAD + k - 2))
                                for h in range(HG):
                                    mm = nc.tensor.matmul(slot(LEAD + k)[32 * h:32 * h + 32, :],
                                                          qr[half][0:KMAX, h, :],
                                                          kt[half][0:KMAX, h, kb * QB:(kb + 1) * QB],
                                                          start=True, stop=True)
                                mm.then_inc(item_made, 1)
                                k += 1
                            pe.wait_ge(reg_max_packed, it * 2 + (half + 1))
                            pe.wait_ge(item_used, it * BODY + (LEAD + k - 2))
                            nc.tensor.transpose(slot(LEAD + k)[0:2, 0:P], reg_packed[:, :], ident[:, :])\
                              .then_inc(item_made, 1)
                            k += 1
                    if 0 <= pos - LAG < NSTEP:
                        s = pos - LAG
                        u, half, i, j = steps[s]
                        pe.wait_ge(exp_done, it * (2 * NSTEP) + 2 * (s + 1))
                        if j == 0 and u > 0:
                            pe.wait_ge(o_copied, it * NUNIT + u)
                        if i == REG_UNIT:
                            for jj in range(KTILES):
                                for h in range(HG):
                                    c = ((jj % 8) * HG + h) * 8
                                    mm = nc.tensor.matmul(o_ps[32 * h:32 * h + VW, 0:8], vt[half][:, jj, h, :],
                                                          prob[:, s % PRING, jj // 8, c:c + 8],
                                                          start=(jj == 0), stop=(jj == KTILES - 1))
                        else:
                            lo = P * (j - 4 * i) if causal and j >= 4 * i else 0
                            for h in range(HG):
                                mm = nc.tensor.matmul(o_ps[32 * h:32 * h + VW, lo:QB], vt[half][:, j, h, :],
                                                      prob[:, s % PRING, h, lo:QB],
                                                      start=(j == 0), stop=(s in last_step))
                        mm.then_inc(pv_done, 1)
                    if pos - LAG - 1 in last_step:
                        u = last_step[pos - LAG - 1]
                        pe.wait_ge(o_copied, it * NUNIT + (u + 1))
                        pe.wait_ge(item_used, it * BODY + (LEAD + k - 2))
                        if units[u][1] == REG_UNIT:
                            mm = nc.tensor.transpose(slot(LEAD + k)[0:8, 0:P], o_sb[:, u % 2, 0:8], ident[:, :])
                        else:
                            for t in range(4):
                                mm = nc.tensor.transpose(slot(LEAD + k)[:, t * P:(t + 1) * P],
                                                         o_sb[:, u % 2, t * P:(t + 1) * P], ident[:, :])
                        mm.then_inc(item_made, 1)
                        k += 1
                    if pos in last_step and units[last_step[pos]][1] != REG_UNIT:
                        turn_max(LEAD + k, it * MAIN + (2 + main), it * BODY + (LEAD + k - 2))
                        k += 1
                assert k == BODY and e == 2 * NSTEP and main == MAIN

        @block.scalar
        def _(act):
            with act.Fori(0, NBODY) as it:
                e = 0
                for pos in range(NSTEP + LAG + 2):
                    if pos < NSTEP:
                        u, half, i, j = steps[pos]
                        lo = P * (j - 4 * i) if causal and j >= 4 * i else 0
                        if pos >= PRING:
                            act.wait_ge(pv_done, it * NSTEP + (pos - PRING + 1))
                        for two in range(2):
                            act.wait_ge(score_made, it * (2 * NSTEP) + (e + 1))
                            if i == REG_UNIT:
                                nc.scalar.activation(prob[:, pos % PRING, two, 0:256], score[:, e % 2, 0, 0:256],
                                                     ACT.Exp, scale=SCALE).then_inc(exp_done, 1)
                            else:
                                nc.scalar.activation(prob[:, pos % PRING, 2 * two:2 * two + 2, lo:QB],
                                                     score[:, e % 2, :, lo:QB], ACT.Exp,
                                                     scale=SCALE).then_inc(exp_done, 1)
                            e += 1
                    if pos - LAG in last_step:
                        u = last_step[pos - LAG]
                        w = 8 if units[u][1] == REG_UNIT else QB
                        act.wait_ge(pv_done, it * NSTEP + (pos - LAG + 1))
                        nc.scalar.copy(o_sb[:, u % 2, 0:w], o_ps[:, 0:w]).then_inc(o_copied, 1)

        @block.vector
        def _(dve):
            nc.vector.memset(o_ps[:, :], 0.0).then_inc(cleared, 1)
            for s in range(2):
                dve.sem_inc(y_stored[s], 16)

            def reduce_item(k, i, h, t, kb, made):
                dve.wait_ge(item_made, made)
                w = P * (t + 1) if causal and kb == i else QB
                nc.vector.tensor_reduce(part_max[:, 4 * h + t, kb:kb + 1], small[(k - LEAD) % 3][:, 0:w], AX.X,
                                        ALU.max).then_inc(item_used, 1)

            def pack(parts_ap, minus, high, out_ap, reduced, step, packed_sem):
                dve.wait_ge(item_used, reduced)
                nc.vector.tensor_reduce(minus, parts_ap, AX.X, ALU.max, negate=True).then_inc(step_done, 1)
                dve.wait_ge(step_done, step)
                nc.vector.tensor_copy(high, minus).then_inc(step_done, 1)
                dve.wait_ge(step_done, step + 1)
                nc.vector.tensor_copy(out_ap[0], high)
                nc.vector.tensor_tensor(out_ap[1], minus, high, ALU.subtract).then_inc(packed_sem, 1)

            def turned_out(k, made, rows):
                dve.wait_ge(item_made, made)
                if rows is not None:
                    dve.wait_ge(rows_in, rows)
                nc.vector.tensor_copy(turned[:, :], small[(k - LEAD) % 3][0:32, 0:P]).then_inc(item_used, 1)

            k = 0
            for i in range(2):
                for h, t, kb in max_blocks(causal, i):
                    reduce_item(k, i, h, t, kb, k + 1)
                    k += 1
                pack(part_max[:, :, 0:i + 1] if causal else part_max[:, :, :], minus_max[:, :], high_max[:, :],
                     (packed[:, 0, :], packed[:, 1, :]), k, 2 * i + 1, max_packed)
                turned_out(k, k + 1, ROWS_DMA * i if i else None)
                k += 1
            with dve.Fori(0, NBODY) as it:
                k, c, main = 0, 0, 0
                for pos in range(NSTEP + LAG + 2):
                    if pos < NSTEP:
                        u, half, i, j = steps[pos]
                        if i != REG_UNIT:
                            _, ahead_i, blocks = max_share(causal, units, steps, last_step, pos)
                            for h, t, kb in blocks:
                                reduce_item(LEAD + k, ahead_i, h, t, kb, it * BODY + (LEAD + k + 1))
                                k += 1
                            if pos in last_step:
                                pack(part_max[:, :, 0:ahead_i + 1] if causal else part_max[:, :, :],
                                     minus_max[:, :], high_max[:, :], (packed[:, 0, :], packed[:, 1, :]),
                                     it * BODY + (LEAD + k), it * BODY_STEPS + (LEAD_STEPS + c + 1), max_packed)
                                c += M_STEPS
                        if reg_lead(pos):
                            for kb in range(QBLOCKS):
                                dve.wait_ge(item_made, it * BODY + (LEAD + k + 1))
                                nc.vector.tensor_reduce(reg_part[:, kb:kb + 1], small[k % 3][:, :], AX.X,
                                                        ALU.max).then_inc(item_used, 1)
                                k += 1
                            pack(reg_part[:, :], reg_minus[:, :], reg_high[:, :],
                                 (reg_packed[:, 0:1], reg_packed[:, 1:2]),
                                 it * BODY + (LEAD + k), it * BODY_STEPS + (LEAD_STEPS + c + 1), reg_max_packed)
                            c += M_STEPS
                            dve.wait_ge(item_made, it * BODY + (LEAD + k + 1))
                            nc.vector.tensor_copy(reg_turned[:, :], small[k % 3][0:2, 0:P]).then_inc(item_used, 1)
                            k += 1
                    if pos - LAG - 1 in last_step:
                        u = last_step[pos - LAG - 1]
                        dve.wait_ge(item_made, it * BODY + (LEAD + k + 1))
                        reg = units[u][1] == REG_UNIT
                        rows, heads = (8, HG) if reg else (P, 4 * HG)
                        o = small[k % 3][0:rows, 0:32 * heads].rearrange("p (a e) -> p a e", e=32)
                        nc.vector.reciprocal(inv[0:rows, u % 2, 0:heads], o[:, :, D]).then_inc(step_done, 1)
                        c += 1
                        dve.wait_ge(step_done, it * BODY_STEPS + (LEAD_STEPS + c))
                        dve.wait_ge(y_stored[u % 2], it * (8 * NUNIT) + 16 * (u // 2 + 1))
                        nc.vector.scalar_tensor_tensor(
                            y_sb[0:rows, u % 2, 0:heads, :], o[:, :, 0:D],
                            const["beta"][0:rows, :] if causal else 1.0,
                            inv[0:rows, u % 2, 0:heads].unsqueeze(2).broadcast_to([rows, heads, D]),
                            ALU.mult, ALU.mult).then_inc(item_used, 1)
                        k += 1
                    if pos in last_step and units[last_step[pos]][1] != REG_UNIT:
                        main += 1
                        turned_out(LEAD + k, it * BODY + (LEAD + k + 1), it * (ROWS_DMA * MAIN) + ROWS_DMA * (main + 1))
                        k += 1
                assert k == BODY and c == BODY_STEPS


def refine_rsqrt(dve, sem, at, y, v, t):
    nc_v = dve
    nc_v.tensor_tensor(t, y, y, ALU.mult).then_inc(sem, 1)
    dve.wait_ge(sem, at + 1)
    nc_v.tensor_tensor(t, t, v, ALU.mult).then_inc(sem, 1)
    dve.wait_ge(sem, at + 2)
    nc_v.tensor_scalar(t, t, -0.5, 1.5, ALU.mult, ALU.add).then_inc(sem, 1)
    dve.wait_ge(sem, at + 3)
    nc_v.tensor_tensor(y, y, t, ALU.mult).then_inc(sem, 1)
    dve.wait_ge(sem, at + 4)


def constants(nc, sems, sb, w_attn, alpha, beta, gamma, g_info, w_qkv, w_proj, b_proj):
    c = {
        "ident": sb("ident", [P, P], F32), "ident_bf": sb("ident_bf", [P, P], BF16),
        "mask_max": sb("mask_max", [P, P], BF16), "mask_exp": sb("mask_exp", [P, P], BF16),
        "ones": sb("ones", [P, P], F32), "upto": sb("upto", [P, P], F32),
        "bias": sb("bias", [P, C], F32), "qg": sb("qg", [P, H, D], F32),
        "alpha": sb("alpha", [P, 1], F32), "beta": sb("beta", [P, 1], F32), "gamma": sb("gamma", [P, 1], F32),
        "share": sb("share", [P, KTILES], F32), "eps": sb("eps", [P, 1], F32),
        "w_a": sb("w_a", [P, KC, 2 * C], F32), "w_f": sb("w_f", [P, KC, 3 * C], F32),
        "w_p": sb("w_p", [P, KC, C], F32),
    }
    with ExitStack() as ctx:
        w_rows = ctx.enter_context(nc.sbuf_tensor("w_rows", [P, 4, C], F32))
        sq = ctx.enter_context(nc.sbuf_tensor("sq", [P, H, D], F32))
        n2 = ctx.enter_context(nc.sbuf_tensor("n2", [P, H], F32))
        y = ctx.enter_context(nc.sbuf_tensor("y", [P, H], F32))
        t = ctx.enter_context(nc.sbuf_tensor("t", [P, H], F32))
        turned = ctx.enter_context(nc.psum_tensor("turned_w", [P, KC, 2 * C], F32))
        w_in = sems.enter_context(nc.semaphore("const_w_in"))
        rows_in = sems.enter_context(nc.semaphore("const_rows_in"))
        filled = sems.enter_context(nc.semaphore("const_filled"))
        shaped = sems.enter_context(nc.semaphore("const_shaped"))
        w_turned = sems.enter_context(nc.semaphore("const_w_turned"))
        rooted = sems.enter_context(nc.semaphore("const_rooted"))
        done = sems.enter_context(nc.semaphore("const_steps"))
        block = ctx.enter_context(nc.Block())

        @block.sync
        def _(sp):
            sp.dma_start(w_rows[:, :, :], w_attn.rearrange("(m p) c -> p m c", p=P)).then_inc(w_in, 16)
            sp.dma_start(c["bias"][:, :], b_proj.partition_broadcast(P)).then_inc(rows_in, 16)
            sp.dma_start(c["qg"][:, :, :].rearrange("p h d -> p (h d)"), g_info[0, 0, :].partition_broadcast(P))\
              .then_inc(rows_in, 16)
            for name, ap in (("alpha", alpha), ("beta", beta), ("gamma", gamma)):
                sp.dma_start(c[name][:, :], ap.partition_broadcast(P)).then_inc(rows_in, 16)
            sp.dma_start(c["w_f"][:, :, :], w_qkv.rearrange("(k p) o -> p k o", p=P)).then_inc(rows_in, 16)
            sp.dma_start(c["w_p"][:, :, :], w_proj.rearrange("(k p) o -> p k o", p=P)).then_inc(rows_in, 16)
            sp.wait_ge(rows_in, 16 * 7)

        @block.gpsimd
        def _(pool):
            for name, value in (("ident", 0.0), ("ident_bf", 0.0), ("mask_max", 0.0), ("mask_exp", 0.0),
                                ("upto", 1.0), ("ones", 1.0), ("eps", EPS)):
                nc.gpsimd.memset(c[name][:, :], value).then_inc(filled, 1)
            pool.wait_ge(filled, 7)
            for name, sign, op, fill in (("ident", 1, ALU.not_equal, 1.0), ("ident_bf", 1, ALU.not_equal, 1.0),
                                         ("mask_max", 1, ALU.is_ge, MASKED), ("mask_exp", -1, ALU.is_ge, MASKED),
                                         ("upto", -1, ALU.is_ge, 0.0)):
                nc.gpsimd.affine_select(out=c[name][:, :], in_=c[name][:, :], compare_op=op, fill=fill, base=0,
                                        pattern=[[-sign, P]], channel_multiplier=sign).then_inc(shaped, 1)
            nc.gpsimd.iota(c["share"][:, :], pattern=[[P, KTILES]], base=1, channel_multiplier=1,
                           allow_small_or_imprecise_dtypes=True).then_inc(shaped, 1)

        @block.tensor
        def _(pe):
            pe.wait_ge(w_in, 16)
            pe.wait_ge(shaped, 1)
            for k in range(KC):
                for m in range(4):
                    mm = nc.tensor.transpose(turned[:, k, m * P:(m + 1) * P], w_rows[:, m, k * P:(k + 1) * P],
                                             c["ident"][:, :])
            mm.then_inc(w_turned, 1)

        @block.scalar
        def _(act):
            act.wait_ge(w_turned, 1)
            for k in range(KC):
                nc.scalar.copy(c["w_a"][:, k, :], turned[:, k, :])
            act.wait_ge(done, 2)
            nc.scalar.activation(y[:, :], n2[:, :], ACT.Sqrt).then_inc(rooted, 1)

        @block.vector
        def _(dve):
            dve.wait_ge(rows_in, 16 * 7)
            nc.vector.tensor_tensor(sq[:, :, :], c["qg"][:, :, :], c["qg"][:, :, :], ALU.mult).then_inc(done, 1)
            dve.wait_ge(done, 1)
            nc.vector.tensor_reduce(n2[:, :], sq[:, :, :], AX.X, ALU.add).then_inc(done, 1)
            dve.wait_ge(rooted, 1)
            nc.vector.reciprocal(y[:, :], y[:, :]).then_inc(done, 1)
            dve.wait_ge(done, 3)
            refine_rsqrt(dve, done, 3, y[:, :], n2[:, :], t[:, :])
            nc.vector.tensor_tensor(c["qg"][:, :, :], c["qg"][:, :, :],
                                    y[:, :].unsqueeze(2).broadcast_to([P, H, D]), ALU.mult).then_inc(done, 1)
            dve.wait_ge(shaped, 6)
            nc.vector.reciprocal(c["share"][:, :], c["share"][:, :]).then_inc(done, 1)
            dve.wait_ge(done, 9)
            nc.vector.tensor_scalar(c["share"][:, :], c["share"][:, :], c["gamma"][:, :], -1.0, ALU.mult,
                                    ALU.mult).then_inc(done, 1)
    return c


def prepare(nc, sems, x, parts, values, base_out, dots, norms, const):
    MT = 8
    with ExitStack() as ctx:
        def sb(name, shape, dt=F32):
            return ctx.enter_context(nc.sbuf_tensor(f"prep_{name}", shape, dt))

        def ps(name, shape):
            return ctx.enter_context(nc.psum_tensor(f"prep_{name}", shape, F32))

        def sem(name):
            return sems.enter_context(nc.semaphore(f"prep_{name}"))

        xs = sb("xs", [P, 2, 4, C])
        xn = sb("xn", [P, 2, 4, C])
        stats = sb("stats", [P, 4, 6])
        mv = sb("mv", [P, 4, 2])
        var = sb("var", [P, 4])
        rstd = sb("rstd", [P, 4])
        newton = sb("newton", [P, 4])
        xn_t = sb("xn_t", [P, KC, QB])
        acc = sb("acc", [P, 2, 4, C])
        base = sb("base", [P, 2, 4, C])
        whole = sb("whole", [P, 2, QB])
        rest = sb("rest", [P, 2, QB])
        split = sb("split", [P, 4, 3, QB], BF16)
        qs = sb("qs", [P, 2, H, D])
        prod = sb("prod", [P, 2, H, D])
        square = sb("square", [P, 2, H, D])
        v_a = sb("v_a", [P, 2, GPB, 4, HG, VW])
        v_f = sb("v_f", [P, 2, GPB, 4, HG, VW])
        p_turn = ps("p_turn", [P, KC, QB])
        p_mean = ps("p_mean", [P, 2, C])
        p_proj = ps("p_proj", [P, 2, QB])
        p_qv = ps("p_qv", [P, 2, 2 * C])

        x_in = [sem(f"x_in{p}") for p in range(2)]
        x_free = sem("x_free")
        stat = sem("stat")
        std_asked = sem("std_asked")
        std_made = sem("std_made")
        xn_made = sem("xn_made")
        turn_made = sem("turn_made")
        turn_copied = sem("turn_copied")
        acc_step = sem("acc_step")
        mean_made = sem("mean_made")
        mean_used = sem("mean_used")
        base_begun = sem("base_begun")
        base_step = sem("base_step")
        base_stored = [sem(f"base_stored{p}") for p in range(2)]
        proj_made = sem("proj_made")
        whole_made = sem("whole_made")
        high_made = sem("high_made")
        rest_made = sem("rest_made")
        mid_made = sem("mid_made")
        low_made = sem("low_made")
        split_out = [sem(f"split_out{s}") for s in range(4)]
        qv_made = sem("qv_made")
        q_copied = sem("q_copied")
        v_copied = sem("v_copied")
        sim_step = sem("sim_step")
        sim_done = sem("sim_done")
        v_a_made = sem("v_a_made")
        ones_set = sem("ones_set")
        v_out = [sem(f"v_out{p}") for p in range(2)]

        x_v = x.rearrange("b (c t p) e -> (b c) p t e", p=P, t=4)
        passed_sp = sem("passed_sp")
        passed_pool = sem("passed_pool")
        passed_dve = sem("passed_dve")
        block = ctx.enter_context(nc.Block())

        @block.sync
        def _(sp):
            for p in range(2):
                sp.dma_start(xs[:, p, :, :], x_v[p]).then_inc(x_in[p], 16)
            with sp.Fori(0, B) as b:
                for c in range(4):
                    par, G = c % 2, b * 4 + c
                    wait_apart(sp, x_free, G + 1, passed_sp)
                    sp.dma_start(xs[:, par, :, :], x_v[bass.ds((G + 2) % CHUNKS, 1)]
                                 .rearrange("o p t e -> (o p) t e")).then_inc(x_in[par], 16)
                    for m in range(MT):
                        wait_apart(sp, low_made, b * (4 * MT) + (MT * c + m + 1 + 2), passed_sp)
                        sp.dma_start(parts[m // 2][:, bass.ds(b * C + (m % 2) * P, P), c * QB:(c + 1) * QB]
                                     .rearrange("r p t -> p r t"), split[:, m % 4, :, :])\
                          .then_inc(split_out[m % 4], 16)
                    wait_apart(sp, base_step, b * 20 + (5 * c + 5), passed_sp)
                    sp.dma_start(base_out[bass.ds(G, 1)].rearrange("o p e -> (o p) e"),
                                 base[:, par, :, :].rearrange("p t e -> p (t e)")).then_inc(base_stored[par], 16)
                    wait_apart(sp, v_a_made, G + 1, passed_sp)
                    wait_apart(sp, v_copied, b * 16 + (4 * c + 4 + 2), passed_sp)
                    for a, v in ((0, v_a), (1, v_f)):
                        sp.dma_start(values[a][bass.ds(b * GPB, GPB), :, 4 * c * HG * VW:4 * (c + 1) * HG * VW]
                                     .rearrange("g p y -> p g y"),
                                     v[:, par, :, :, :, :].rearrange("p g t h e -> p g (t h e)"))\
                          .then_inc(v_out[par], 16)
            for p in range(2):
                sp.wait_ge(x_in[p], 16 * (CHUNKS // 2 + 1))
                sp.wait_ge(base_stored[p], 16 * (CHUNKS // 2 + 1))
                sp.wait_ge(v_out[p], 32 * (CHUNKS // 2 + 1))
            for s in range(4):
                sp.wait_ge(split_out[s], 16 * (2 * CHUNKS + 1))

        @block.tensor
        def _(pe):
            with pe.Fori(0, B) as b:
                for c in range(4):
                    par, G = c % 2, b * 4 + c
                    pe.wait_ge(xn_made, G + 1)
                    for k in range(KC):
                        for t in range(4):
                            mm = nc.tensor.transpose(p_turn[:, k, t * P:(t + 1) * P],
                                                     xn[:, par, t, k * P:(k + 1) * P], const["ident"][:, :])
                    mm.then_inc(turn_made, 1)
                    pe.wait_ge(acc_step, b * 16 + (4 * c + 3 + 1))
                    for two in range(2):
                        pe.wait_ge(mean_used, b * 8 + (2 * c + two + 1))
                        for t in range(2 * two, 2 * two + 2):
                            nc.tensor.matmul(p_mean[:, t % 2, :], const["upto"][:, :], xn[:, par, t, :],
                                             start=True, stop=False)
                            mm = nc.tensor.matmul(p_mean[:, t % 2, :], const["ones"][:, :], acc[:, par, t, :],
                                                  start=False, stop=True)
                        mm.then_inc(mean_made, 1)
                    pe.wait_ge(turn_copied, b * 8 + (2 * c + 2))
                    for m in range(MT):
                        w = const["w_a" if m < 4 else "w_f"]
                        pe.wait_ge(whole_made, b * (4 * MT) + (MT * c + m + 1))
                        for k in range(KC):
                            mm = nc.tensor.matmul(p_proj[:, m % 2, :], w[:, k, (m % 4) * P:(m % 4 + 1) * P],
                                                  xn_t[:, k, :], start=(k == 0), stop=(k == KC - 1))
                        mm.then_inc(proj_made, 1)
                    w_qv = const["w_f"][:, :, :].rearrange("p k (s o) -> p k s o", o=C)
                    for t in range(4):
                        pe.wait_ge(v_copied, b * 16 + (4 * c + t + 1))
                        for k in range(KC):
                            mm = nc.tensor.matmul(p_qv[:, t % 2, :], xn_t[:, k, t * P:(t + 1) * P],
                                                  w_qv[:, k, 0:3:2, :], start=(k == 0), stop=(k == KC - 1))
                        mm.then_inc(qv_made, 1)

        @block.scalar
        def _(act):
            act.sem_inc(whole_made, 2)
            act.sem_inc(v_copied, 2)

            def root(asked):
                act.wait_ge(std_asked, asked)
                nc.scalar.activation(rstd[:, :], var[:, :], ACT.Sqrt).then_inc(std_made, 1)

            root(1)
            with act.Fori(0, B) as b:
                for c in range(4):
                    par, G = c % 2, b * 4 + c
                    act.wait_ge(turn_made, G + 1)
                    for k in range(KC):
                        nc.scalar.copy(xn_t[:, k, :], p_turn[:, k, :]).then_inc(turn_copied, 1)
                    for m in range(MT):
                        act.wait_ge(proj_made, b * (4 * MT) + (MT * c + m + 1))
                        act.wait_ge(rest_made, b * (4 * MT) + (MT * c + m + 1))
                        nc.scalar.copy(whole[:, m % 2, :], p_proj[:, m % 2, :]).then_inc(whole_made, 1)
                        if m == 4:
                            root(G + 2)
                    act.wait_ge(v_out[par], b * 64 + 32 * (c // 2 + 1))
                    if c == 0:
                        act.wait_ge(ones_set, 2)
                    for t in range(4):
                        act.wait_ge(qv_made, b * 16 + (4 * c + t + 1))
                        act.wait_ge(sim_done, b * 16 + (4 * c + t + 1))
                        nc.scalar.copy(qs[:, t % 2, :, :].rearrange("p h d -> p (h d)"),
                                       p_qv[:, t % 2, 0:C]).then_inc(q_copied, 1)
                        nc.scalar.copy(v_f[:, par, :, t, :, 0:D],
                                       p_qv[:, t % 2, C:2 * C].rearrange("p (g h d) -> p g h d", g=GPB, d=D))\
                          .then_inc(v_copied, 1)

        @block.gpsimd
        def _(pool):
            pool.sem_inc(low_made, 2)
            for v in (v_a, v_f):
                nc.gpsimd.memset(v[:, :, :, :, :, :], 1.0).then_inc(ones_set, 1)
            nc.gpsimd.memset(acc[:, 0, 0, :], 0.0).then_inc(acc_step, 1)
            pool.wait_ge(ones_set, 2)
            with pool.Fori(0, B) as b:
                for c in range(4):
                    par, G = c % 2, b * 4 + c
                    pool.wait_ge(xn_made, G + 1)
                    for t in range(4):
                        wait_apart(pool, acc_step, b * 16 + (4 * c + t + 1), passed_pool)
                        if t < 3 or c < 3:
                            nxt = acc[:, par, t + 1, :] if t < 3 else acc[:, 1 - par, 0, :]
                            nc.gpsimd.tensor_tensor(nxt, acc[:, par, t, :], xn[:, par, t, :], ALU.add)\
                              .then_inc(acc_step, 1)
                        else:
                            nc.gpsimd.memset(acc[:, 0, 0, :], 0.0).then_inc(acc_step, 1)
                    pool.wait_ge(base_stored[par], b * 32 + 16 * (c // 2 + 1))
                    nc.gpsimd.tensor_tensor(base[:, par, :, :], xs[:, par, :, :],
                                            const["bias"][:, :].unsqueeze(1).broadcast_to([P, 4, C]), ALU.add)\
                      .then_inc(base_begun, 1)
                    pool.wait_ge(base_begun, G + 1)
                    pool.sem_inc(x_free, 1)
                    wait_apart(pool, v_out[par], b * 64 + 32 * (c // 2 + 1), passed_pool)
                    for t in range(4):
                        cp = nc.gpsimd.tensor_copy(v_a[:, par, :, t, :, 0:D],
                                                   xn[:, par, t, :].rearrange("p (g h d) -> p g h d", g=GPB, d=D))
                    cp.then_inc(v_a_made, 1)
                    for m in range(MT):
                        pool.wait_ge(mid_made, b * (4 * MT) + (MT * c + m + 1))
                        nc.gpsimd.tensor_tensor(split[:, m % 4, 2, :], rest[:, m % 2, :], split[:, m % 4, 1, :],
                                                ALU.subtract).then_inc(low_made, 1)

        @block.vector
        def _(dve):
            dve.sem_inc(mean_used, 1)
            dve.sem_inc(rest_made, 2)
            dve.sem_inc(sim_done, 2)
            for p in range(2):
                dve.sem_inc(base_stored[p], 16)
                dve.sem_inc(v_out[p], 32)
            for s in range(4):
                dve.sem_inc(split_out[s], 16)
            STAT = 9

            def norm(par, x_there, G, base_stat):
                dve.wait_ge(x_in[par], x_there)
                for t in range(4):
                    bn = nc.vector.bn_stats(stats[:, t, :], xs[:, par, t, :])
                bn.then_inc(stat, 1)
                wait_apart(dve, stat, base_stat + 1, passed_dve)
                for t in range(4):
                    bn = nc.vector.bn_aggr(mv[:, t, :], stats[:, t, :])
                bn.then_inc(stat, 1)
                dve.wait_ge(stat, base_stat + 2)
                nc.vector.tensor_scalar(var[:, :], mv[:, :, 1], EPS, None, ALU.add).then_inc(std_asked, 1)
                dve.wait_ge(std_made, G + 1)
                dve.wait_ge(std_asked, G + 1)
                nc.vector.reciprocal(rstd[:, :], rstd[:, :]).then_inc(stat, 1)
                dve.wait_ge(stat, base_stat + 3)
                refine_rsqrt(dve, stat, base_stat + 3, rstd[:, :], var[:, :], newton[:, :])
                for t in range(4):
                    ts = nc.vector.tensor_scalar(xn[:, par, t, :], xs[:, par, t, :], mv[:, t, 0:1], rstd[:, t:t + 1],
                                                 ALU.subtract, ALU.mult)
                ts.then_inc(xn_made, 1)

            norm(0, 16, 0, 0)
            with dve.Fori(0, B) as b:
                for c in range(4):
                    par, G = c % 2, b * 4 + c
                    dve.wait_ge(base_begun, G + 1)
                    dve.wait_ge(xn_made, G + 1)
                    nc.vector.scalar_tensor_tensor(base[:, par, :, :].rearrange("p t e -> p (t e)"),
                                                   xn[:, par, :, :].rearrange("p t e -> p (t e)"),
                                                   const["alpha"][:, :],
                                                   base[:, par, :, :].rearrange("p t e -> p (t e)"),
                                                   ALU.mult, ALU.add).then_inc(base_step, 1)
                    dve.wait_ge(base_step, b * 20 + (5 * c + 1))
                    for two in range(2):
                        dve.wait_ge(mean_made, b * 8 + (2 * c + two + 1))
                        for t in range(2 * two, 2 * two + 2):
                            st = nc.vector.scalar_tensor_tensor(
                                base[:, par, t, :], p_mean[:, t % 2, :], const["share"][:, 4 * c + t:4 * c + t + 1],
                                base[:, par, t, :], ALU.mult, ALU.add).then_inc(base_step, 1)
                        dve.wait_ge(base_step, b * 20 + (5 * c + 2 * two + 3))
                        dve.sem_inc(mean_used, 1)
                    for m in range(MT):
                        i = MT * c + m
                        dve.wait_ge(split_out[m % 4], b * 128 + 16 * (2 * c + m // 4 + 1))
                        dve.wait_ge(whole_made, b * (4 * MT) + (i + 1 + 2))
                        nc.vector.tensor_copy(split[:, m % 4, 0, :], whole[:, m % 2, :]).then_inc(high_made, 1)
                        dve.wait_ge(high_made, b * (4 * MT) + (i + 1))
                        dve.wait_ge(low_made, b * (4 * MT) + (i + 1))
                        nc.vector.tensor_tensor(rest[:, m % 2, :], whole[:, m % 2, :], split[:, m % 4, 0, :],
                                                ALU.subtract).then_inc(rest_made, 1)
                        dve.wait_ge(rest_made, b * (4 * MT) + (i + 1 + 2))
                        nc.vector.tensor_copy(split[:, m % 4, 1, :], rest[:, m % 2, :]).then_inc(mid_made, 1)
                        if m == 4:
                            norm(1 - par, b * 32 + 16 * ((c + 1) // 2 + 1), G + 1, b * (4 * 7) + 7 * (c + 1))
                    for t in range(4):
                        i = 4 * c + t
                        dve.wait_ge(q_copied, b * 16 + (i + 1))
                        nc.vector.tensor_tensor(prod[:, t % 2, :, :], qs[:, t % 2, :, :], const["qg"][:, :, :],
                                                ALU.mult).then_inc(sim_step, 1)
                        nc.vector.tensor_tensor(square[:, t % 2, :, :], qs[:, t % 2, :, :], qs[:, t % 2, :, :],
                                                ALU.mult).then_inc(sim_step, 1)
                        dve.wait_ge(sim_step, b * 32 + (2 * i + 2))
                        nc.vector.tensor_reduce(dots[:, bass.ds(b * KTILES + i, 1), :]
                                                .rearrange("p o h -> p (o h)"), prod[:, t % 2, :, :], AX.X, ALU.add)
                        nc.vector.tensor_reduce(norms[:, bass.ds(b * KTILES + i, 1), :]
                                                .rearrange("p o h -> p (o h)"), square[:, t % 2, :, :], AX.X,
                                                ALU.add).then_inc(sim_done, 1)


def classify(nc, sems, dots, norms, masks, reg_rows, const):
    NT = B * KTILES
    with ExitStack() as ctx:
        def sb(name, shape, dt=F32):
            return ctx.enter_context(nc.sbuf_tensor(f"class_{name}", shape, dt))

        root = sb("root", [P, NT, H])
        newton = sb("newton", [P, NT, H])
        sim = sb("sim", [P, NT])
        edge = sb("edge", [P, 2, NT])
        ends = sb("ends", [P, 2])
        both = sb("both", [P, 2])
        width = sb("width", [P, 1])
        pos = sb("pos", [P, NT])
        rows = sb("rows", [P, 4, NT])
        rows_t = sb("rows_t", [P, 2, P], BF16)
        reg = sb("reg", [2, P], BF16)
        p_rows = ctx.enter_context(nc.psum_tensor("p_rows", [P, 2, P], F32))
        rooted = sems.enter_context(nc.semaphore("class_rooted"))
        step = sems.enter_context(nc.semaphore("class_step"))
        ends_made = sems.enter_context(nc.semaphore("class_ends_made"))
        ends_shared = sems.enter_context(nc.semaphore("class_ends_shared"))
        rows_made = sems.enter_context(nc.semaphore("class_rows_made"))
        rows_turned = sems.enter_context(nc.semaphore("class_rows_turned"))
        rows_ready = sems.enter_context(nc.semaphore("class_rows_ready"))
        stored = sems.enter_context(nc.semaphore("class_stored"))
        block = ctx.enter_context(nc.Block())

        @block.scalar
        def _(act):
            nc.scalar.activation(root[:, :, :], norms[:, :, :], ACT.Sqrt).then_inc(rooted, 1)

        @block.gpsimd
        def _(pool):
            pool.wait_ge(ends_made, 1)
            nc.gpsimd.partition_all_reduce(both[:, :], ends[:, :], P, bass.bass_isa.ReduceOp.max)\
              .then_inc(ends_shared, 1)

        @block.tensor
        def _(pe):
            pe.wait_ge(rows_made, 1)
            for a in range(2):
                mm = nc.tensor.transpose(p_rows[:, a, :], rows[:, 2 * a:2 * a + 2, :].rearrange("p k t -> p (k t)"),
                                         const["ident"][:, :])
            mm.then_inc(rows_turned, 1)

        @block.sync
        def _(sp):
            sp.wait_ge(rows_ready, 1)
            for k in range(4):
                sp.dma_start(masks[k].rearrange("b (t x) -> (b t) x", x=P),
                             rows_t[64 * (k % 2):64 * (k % 2) + 64, k // 2, :]).then_inc(stored, 16)
            sp.dma_start(reg_rows, reg[:, :]).then_inc(stored, 16)
            sp.wait_ge(stored, 16 * 5)

        @block.vector
        def _(dve):
            count = [0]

            def link(ins):
                ins.then_inc(step, 1)
                count[0] += 1
                dve.wait_ge(step, count[0])

            link(nc.vector.memset(reg[:, :], 0.0))
            link(nc.vector.memset(reg[0:1, :], MASKED))
            dve.wait_ge(rooted, 1)
            link(nc.vector.reciprocal(root[:, :, :], root[:, :, :]))
            refine_rsqrt(dve, step, count[0], root[:, :, :], norms[:, :, :], newton[:, :, :])
            count[0] += 4
            link(nc.vector.tensor_tensor(root[:, :, :], root[:, :, :], dots[:, :, :], ALU.mult))
            link(nc.vector.tensor_reduce(sim[:, :], root[:, :, :], AX.X, ALU.add))
            link(nc.vector.tensor_scalar(sim[:, :], sim[:, :], 1.0 / H, None, ALU.mult))
            nc.vector.tensor_copy(edge[:, 0, :], sim[:, :])
            link(nc.vector.tensor_scalar(edge[:, 1, :], sim[:, :], -1.0, None, ALU.mult))
            link(nc.vector.memset(edge[0:REG, :, 0:NT:KTILES], -3e38))
            nc.vector.tensor_reduce(ends[:, :], edge[:, :, :], AX.X, ALU.max).then_inc(ends_made, 1)
            dve.wait_ge(ends_shared, 1)
            link(nc.vector.tensor_tensor(width[:, :], both[:, 0:1], both[:, 1:2], ALU.add))
            link(nc.vector.reciprocal(width[:, :], width[:, :]))
            link(nc.vector.tensor_scalar(sim[:, :], sim[:, :], both[:, 1:2], width[:, :], ALU.add, ALU.mult))
            link(nc.vector.tensor_scalar(pos[:, :], sim[:, :], 0.9, None, ALU.is_gt))
            nc.vector.tensor_copy(rows[:, 0, :], pos[:, :])
            link(nc.vector.tensor_scalar(rows[:, 1, :], pos[:, :], -1.0, 1.0, ALU.mult, ALU.add))
            link(nc.vector.memset(rows[0:REG, 0:2, 0:NT:KTILES], 0.0))
            link(nc.vector.memset(pos[0:REG, 0:NT:KTILES], 1.0))
            nc.vector.tensor_scalar(rows[:, 2, :], pos[:, :], -MASKED, MASKED, ALU.mult, ALU.add)
            nc.vector.tensor_scalar(rows[:, 3, :], pos[:, :], MASKED, None, ALU.mult).then_inc(rows_made, 1)
            dve.wait_ge(rows_turned, 1)
            nc.vector.tensor_copy(rows_t[:, :, :], p_rows[:, :, :]).then_inc(rows_ready, 1)


def finish(nc, sems, base_in, y_a, y_f, y_reg, out, const):
    CAME = 16 * (2 + GPB)
    with ExitStack() as ctx:
        def sb(name, shape):
            return ctx.enter_context(nc.sbuf_tensor(f"fin_{name}", shape, F32))

        def sem(name):
            return sems.enter_context(nc.semaphore(f"fin_{name}"))

        ya = sb("ya", [P, 2, GPB, 4, HG * D])
        yf = sb("yf", [P, 2, 4, GPB, HG * D])
        yr = sb("yr", [8, GPB, HG * D])
        base = sb("base", [P, 2, 4, C])
        yt = sb("yt", [P, KC, QB])
        res = sb("res", [P, 2, 4, C])
        p_turn = ctx.enter_context(nc.psum_tensor("fin_turn", [P, 2, KC, QB], F32))
        p_out = ctx.enter_context(nc.psum_tensor("fin_out", [P, 2, 2, C], F32))
        came = [sem(f"came{p}") for p in range(2)]
        reg_came = sem("reg_came")
        reg_step = sem("reg_step")
        added = sem("added")
        turned = sem("turned")
        copied = sem("copied")
        made = sem("made")
        summed = sem("summed")
        stored = [sem(f"stored{p}") for p in range(2)]
        out_v = out.rearrange("b (c t p) e -> (b c) p t e", p=P, t=4)
        passed_sp = sem("passed_sp")
        block = ctx.enter_context(nc.Block())

        @block.sync
        def _(sp):
            def load(n, par, b, c):
                sp.dma_start(ya[:, par, :, :, :].rearrange("p g t e -> p g (t e)"),
                             y_a[bass.ds(b * GPB, GPB), c].rearrange("g p x -> p g x")).then_inc(came[par], 16)
                for g in range(GPB):
                    sp.dma_start(yf[:, par, :, g, :], y_f[bass.ds(b * GPB + g, 1), c]
                                 .rearrange("o p (t e) -> (o p) t e", t=4)).then_inc(came[par], 16)
                sp.dma_start(base[:, par, :, :].rearrange("p t e -> p (t e)"),
                             base_in[bass.ds(n, 1)].rearrange("o p e -> (o p) e")).then_inc(came[par], 16)

            def load_reg(b_rows):
                sp.dma_start(yr[:, :, :], y_reg[b_rows].rearrange("g r x -> r g x")).then_inc(reg_came, 16)

            load(0, 0, 0, 0)
            load_reg(bass.ds(0, GPB))
            with sp.Fori(0, B) as b:
                for c in range(4):
                    par, G = c % 2, b * 4 + c
                    nxt = (G + 1) % CHUNKS
                    wait_apart(sp, summed, b * 8 + (2 * c + 2), passed_sp)
                    if c < 3:
                        load(nxt, 1 - par, b, c + 1)
                    else:
                        nb = (b + 1) % B
                        load(nxt, 1 - par, nb, 0)
                        load_reg(bass.ds(nb * GPB, GPB))
                    wait_apart(sp, summed, b * 8 + (2 * c + 2 + 2), passed_sp)
                    sp.dma_start(out_v[bass.ds(G, 1)].rearrange("o p t e -> (o p) t e"), res[:, par, :, :])\
                      .then_inc(stored[par], 16)
            sp.wait_ge(came[0], CAME * (CHUNKS // 2 + 1))
            sp.wait_ge(reg_came, 16 * (B + 1))
            for p in range(2):
                sp.wait_ge(stored[p], 16 * (CHUNKS // 2 + 1))

        @block.gpsimd
        def _(pool):
            with pool.Fori(0, B) as b:
                for c in range(4):
                    par = c % 2
                    pool.wait_ge(came[par], b * (2 * CAME) + CAME * (c // 2 + 1))
                    for t in range(4):
                        tt = nc.gpsimd.tensor_tensor(
                            base[:, par, t, :].rearrange("p (g e) -> p g e", g=GPB),
                            base[:, par, t, :].rearrange("p (g e) -> p g e", g=GPB), ya[:, par, :, t, :], ALU.add)
                    tt.then_inc(added, 1)

        @block.tensor
        def _(pe):
            with pe.Fori(0, B) as b:
                for c in range(4):
                    par, G = c % 2, b * 4 + c
                    pe.wait_ge(came[par], b * (2 * CAME) + CAME * (c // 2 + 1))
                    if c == 0:
                        pe.wait_ge(reg_step, b * 2 + 2)
                    for k in range(KC):
                        for t in range(4):
                            mm = nc.tensor.transpose(p_turn[:, par, k, t * P:(t + 1) * P],
                                                     yf[:, par, t, 2 * k:2 * k + 2, :].rearrange("p g e -> p (g e)"), const["ident"][:, :])
                    mm.then_inc(turned, 1)
                    pe.wait_ge(copied, b * 8 + (2 * c + 2))
                    for two in range(2):
                        pe.wait_ge(summed, b * 8 + (2 * c + two + 1))
                        for t in range(2 * two, 2 * two + 2):
                            for k in range(KC):
                                mm = nc.tensor.matmul(p_out[:, two, t % 2, :], yt[:, k, t * P:(t + 1) * P],
                                                      const["w_p"][:, k, :], start=(k == 0), stop=(k == KC - 1))
                        mm.then_inc(made, 1)

        @block.scalar
        def _(act):
            with act.Fori(0, B) as b:
                for c in range(4):
                    par, G = c % 2, b * 4 + c
                    act.wait_ge(turned, G + 1)
                    for k in range(KC):
                        nc.scalar.copy(yt[:, k, :], p_turn[:, par, k, :]).then_inc(copied, 1)

        @block.vector
        def _(dve):
            dve.sem_inc(summed, 2)
            for p in range(2):
                dve.sem_inc(stored[p], 16)
            with dve.Fori(0, B) as b:
                for c in range(4):
                    par, G = c % 2, b * 4 + c
                    if c == 0:
                        dve.wait_ge(came[par], b * (2 * CAME) + CAME)
                        dve.wait_ge(reg_came, b * 16 + 16)
                        nc.vector.tensor_tensor(yf[0:REG, par, 0, :, :], yf[0:REG, par, 0, :, :],
                                                yr[0:REG, :, :], ALU.add).then_inc(reg_step, 1)
                        dve.wait_ge(reg_step, b * 2 + 1)
                        nc.vector.tensor_scalar(yf[0:REG, par, 0, :, :], yf[0:REG, par, 0, :, :], 0.5, None,
                                                ALU.mult).then_inc(reg_step, 1)
                    dve.wait_ge(added, G + 1)
                    dve.wait_ge(stored[par], b * 32 + 16 * (c // 2 + 1))
                    for two in range(2):
                        dve.wait_ge(made, b * 8 + (2 * c + two + 1))
                        nc.vector.tensor_tensor(res[:, par, 2 * two:2 * two + 2, :], p_out[:, two, :, :],
                                                base[:, par, 2 * two:2 * two + 2, :], ALU.add).then_inc(summed, 1)


def build(nc, x, w_attn, alpha, beta, gamma, g_info, w_qkv, w_proj, b_proj, out):
    def dram(name, shape, dt=F32):
        return nc.dram_tensor(name, shape, dt, kind="Internal").ap()

    parts = dram("parts", (4, 3, B * C, T), BF16)
    values = dram("values", (2, GROUPS, P, KTILES * HG * VW))
    base = dram("base", (CHUNKS, P, 4 * C))
    masks = dram("masks", (4, B, T), BF16)
    reg_rows = dram("reg_rows", (2, P), BF16)
    y_a = dram("y_a", (GROUPS, QBLOCKS, P, 4 * HG * D))
    y_f = dram("y_f", (GROUPS, QBLOCKS, P, 4 * HG * D))
    y_reg = dram("y_reg", (GROUPS, 8, HG * D))
    with ExitStack() as ctx:
        def sb(name, shape, dt):
            return ctx.enter_context(nc.sbuf_tensor(name, shape, dt))

        const = constants(nc, ctx, sb, w_attn, alpha, beta, gamma, g_info, w_qkv, w_proj, b_proj)
        with ExitStack() as sims:
            dots = sims.enter_context(nc.sbuf_tensor("dots", [P, B * KTILES, H], F32))
            norms = sims.enter_context(nc.sbuf_tensor("norms", [P, B * KTILES, H], F32))
            prepare(nc, ctx, x, parts, values, base, dots, norms, const)
            classify(nc, ctx, dots, norms, masks, reg_rows, const)
        attend(nc, ctx, True, (parts[0], parts[1]), values[0], None, None, y_a, None, const)
        attend(nc, ctx, False, (parts[2], parts[3]), values[1], masks, reg_rows, y_f, y_reg, const)
        finish(nc, ctx, base, y_a, y_f, y_reg, out, const)


_INS = ["L0_attn_x", "L0_attn_W_attn", "L0_attn_alpha", "L0_attn_beta", "L0_attn_gamma", "L0_ffn_g_info",
        "L0_ffn_W_qkv", "L0_ffn_W_proj", "L0_ffn_b_proj"]


def kernel(**inputs):
    import concourse.bacc as _bacc
    from concourse.bass_utils import run_bass_kernel_spmd as _run

    nc = _bacc.Bacc("TRN2", target_bir_lowering=False, num_devices=1)
    arrays, args = {}, []
    for name in _INS:
        a = np.ascontiguousarray(inputs[name])
        arrays[f"in_{name}"] = a
        args.append(nc.dram_tensor(f"in_{name}", a.shape, mybir.dt.from_np(a.dtype), kind="ExternalInput").ap())
    out = nc.dram_tensor("out_0", (B, T, C), F32, kind="ExternalOutput").ap()
    build(nc, *args, out)
    return _run(nc, [arrays], core_ids=[0]).results[0]["out_0"]
```

```python
from contextlib import ExitStack

import numpy as np

import concourse.bass as bass
from concourse import mybir

F32 = mybir.dt.float32
BF16 = mybir.dt.bfloat16
ALU = mybir.AluOpType
ACT = mybir.ActivationFunctionType
AX = mybir.AxisListType

P = 128
B, T, C = 4, 2048, 256
H = 16
D = C // H
REG = 5
HG = 4
GROUPS = B * H // HG
GPB = H // HG
QB = 512
QBLOCKS = T // QB
KTILES = T // P
CHUNKS = B * QBLOCKS
KC = C // P
VW = D + 1
SPLIT_ROWS = 6 * D
Q_PART = (0, 0, 1, 0, 1, 2)
K_PART = (0, 1, 0, 2, 1, 0)
SCALE = float(D) ** -0.5
MASKED = -(2.0 ** 40)
EPS = 1e-5
LAG = 2
PRING = 4
MAX_AHEAD = 80
REG_UNIT = -1


def wait_apart(engine, sem, value, passed):
    engine.wait_ge(sem, value)
    engine.sem_inc(passed, 1)


def attend_plan(causal):
    units, steps, last_step = [], [], {}
    for half in range(2):
        for i in list(range(QBLOCKS)) + ([] if causal else [REG_UNIT]):
            units.append((half, i))
            n = 1 if i == REG_UNIT else (4 * (i + 1) if causal else KTILES)
            for j in range(n):
                steps.append((len(units) - 1, half, i, j))
            last_step[len(steps) - 1] = len(units) - 1
    return units, steps, last_step


def max_blocks(causal, i):
    return [(h, t, kb) for h in range(HG) for t in range(4) for kb in range((i + 1) if causal else QBLOCKS)]


def max_stream(causal):
    out = []
    for i in range(QBLOCKS):
        blocks = max_blocks(causal, i)
        out += [(i, *blk, n == len(blocks) - 1) for n, blk in enumerate(blocks)]
    return out


def max_share(causal, step):
    _, half, i, j = step
    if i == REG_UNIT:
        return []
    stream = max_stream(causal)
    G = len(stream)
    m, S = (sum(4 * (a + 1) for a in range(i)) + j, 40) if causal else (KTILES * i + j, KTILES * QBLOCKS)
    return [(half if n < G else 1 - half, *stream[n % G])
            for n in range(MAX_AHEAD + G * m // S, MAX_AHEAD + G * (m + 1) // S)]


def units_packed(causal, step):
    return [(half, i) for half, i, _, _, _, last in max_share(causal, step) if last]


def attend(nc, sems, causal, parts, values, masks, reg_rows, result, reg_result, const):
    tag = "causal" if causal else "class"
    units, steps, last_step = attend_plan(causal)
    NSTEP, NUNIT = len(steps), len(units)
    MAIN = sum(i != REG_UNIT for _, i in units)
    MROW = SPLIT_ROWS if causal else SPLIT_ROWS + 2
    KMAX, KEXP = MROW, MROW + 2
    NREG = NUNIT - MAIN
    lead_blocks = max_stream(causal)[:MAX_AHEAD]
    LEAD_UNITS = sum(last for *_, last in lead_blocks)
    LEAD = MAX_AHEAD + LEAD_UNITS
    BODY = sum(len(max_blocks(causal, i)) for _, i in units if i != REG_UNIT) + MAIN + NUNIT + NREG * (QBLOCKS + 1)
    LOADS = 6 * 2 + 1 + (0 if causal else 8 + 6 + 1)
    M_STEPS = 2
    LEAD_STEPS = LEAD_UNITS * M_STEPS
    BODY_STEPS = MAIN * M_STEPS + NREG * M_STEPS + NUNIT
    NBODY = GROUPS // 2
    ROWS_DMA = 16 * 2 * HG

    with ExitStack() as ctx:
        def sb(name, shape, dt):
            return ctx.enter_context(nc.sbuf_tensor(f"{tag}_{name}", shape, dt))

        def ps(name, shape, dt):
            return ctx.enter_context(nc.psum_tensor(f"{tag}_{name}", shape, dt))

        def sem(name):
            return sems.enter_context(nc.semaphore(f"{tag}_{name}"))

        kt = [sb(f"kt{p}", [SPLIT_ROWS + 4, HG, T], BF16) for p in range(2)]
        qt = [sb(f"qt{p}", [SPLIT_ROWS + 4, HG, T], BF16) for p in range(2)]
        qr = [sb(f"qr{p}", [SPLIT_ROWS + 4, HG, 32], BF16) for p in range(2)]
        vt = [sb(f"vt{p}", [P, KTILES, HG, VW], F32) for p in range(2)]
        prob = sb("prob", [P, PRING, HG, QB], F32)
        o_sb = sb("o_sb", [P, 2, QB], F32)
        y_sb = sb("y_sb", [P, 2, 4 * HG, D], F32)
        part_max = sb("part_max", [P, 16, QBLOCKS], F32)
        minus_max = sb("minus_max", [P, 16], F32)
        high_max = sb("high_max", [P, 16], BF16)
        packed = sb("packed", [P, 2, 16], F32)
        turned = sb("turned", [32, P], BF16)
        reg_part = sb("reg_part", [P, QBLOCKS], F32)
        reg_minus = sb("reg_minus", [P, 1], F32)
        reg_high = sb("reg_high", [P, 1], BF16)
        reg_packed = sb("reg_packed", [P, 2], F32)
        reg_turned = sb("reg_turned", [2, P], BF16)
        inv = sb("inv", [P, 2, 16], F32)
        small = [ps(f"small{s}", [P, QB], F32) for s in range(3)]
        score = ps("score", [P, 2, 2, QB], F32)
        o_ps = ps("o_ps", [P, QB], F32)

        loaded = [sem(f"loaded{p}") for p in range(2)]
        ones_set = sem("ones_set")
        cleared = sem("cleared")
        item_made = sem("item_made")
        item_used = sem("item_used")
        step_done = sem("step_done")
        max_packed = sem("max_packed")
        reg_max_packed = sem("reg_max_packed")
        rows_in = sem("rows_in")
        reg_rows_in = sem("reg_rows_in")
        score_made = sem("score_made")
        exp_done = sem("exp_done")
        pv_done = sem("pv_done")
        o_copied = sem("o_copied")
        y_stored = [sem(f"y_stored{s}") for s in range(2)]
        y_free = [sem(f"y_free{s}") for s in range(2)]

        passed_sp = sem("passed_sp")
        passed_pool = sem("passed_pool")
        block = ctx.enter_context(nc.Block())

        def reg_lead(pos):
            return pos < NSTEP and not causal and steps[pos][2] == 0 and steps[pos][3] == 1

        def packed_before(pos):
            done = units_packed(causal, steps[pos - 1]) if 0 < pos <= NSTEP else []
            return done[0] if done else None

        @block.sync
        def _(sp):
            def load(n, par):
                for r in range(6):
                    rows = bass.ds(n * HG * D, HG * D)
                    for dst, part in ((kt[par], parts[1][K_PART[r]]), (qt[par], parts[0][Q_PART[r]])):
                        sp.dma_start(dst[r * D:(r + 1) * D, :, :],
                                     part[rows, :].rearrange("(h d) t -> d h t", d=D)).then_inc(loaded[par], 16)
                    if not causal:
                        sp.dma_start(qr[par][r * D:(r + 1) * D, :, :],
                                     parts[0][Q_PART[r]][rows, 0:32].rearrange("(h d) t -> d h t", d=D))\
                          .then_inc(loaded[par], 16)
                sp.dma_start(vt[par][:, :, :, :].rearrange("p k h e -> p (k h e)"),
                             values[bass.ds(n, 1)].rearrange("o p x -> (o p) x")).then_inc(loaded[par], 16)
                if not causal:
                    for h in range(HG):
                        b = n // 4
                        sp.dma_start(kt[par][SPLIT_ROWS:SPLIT_ROWS + 2, h, :],
                                     masks[0:2, bass.ds(b, 1), :].rearrange("k o t -> k (o t)"))\
                          .then_inc(loaded[par], 16)
                        sp.dma_start(qt[par][SPLIT_ROWS:SPLIT_ROWS + 2, h, :],
                                     masks[2:4, bass.ds(b, 1), :].rearrange("k o t -> k (o t)"))\
                          .then_inc(loaded[par], 16)
                    sp.dma_start(qr[par][SPLIT_ROWS:SPLIT_ROWS + 2, :, :].rearrange("r h q -> r (h q)"),
                                 reg_rows).then_inc(loaded[par], 16)

            def store_rows(par, i, used):
                sp.wait_ge(item_used, used)
                for r in range(2):
                    for h in range(HG):
                        sp.dma_start(qt[par][MROW + r:MROW + r + 1, h, i * QB:(i + 1) * QB],
                                     turned[16 * r + 4 * h:16 * r + 4 * h + 4, :]).then_inc(rows_in, 16)

            sp.wait_ge(ones_set, 2)
            load(0, 0)
            k = 0
            for i, _, _, _, last in lead_blocks:
                k += 1
                if last:
                    k += 1
                    store_rows(0, i, k)
            with sp.Fori(0, NBODY) as it:
                k = 0
                for pos in range(NSTEP + LAG + 2):
                    if pos < NSTEP:
                        u, half, i, j = steps[pos]
                        if i == 1 and j == 0:
                            wait_apart(sp, pv_done, it * NSTEP + pos, passed_sp)
                            load((it * 2 + (half + 1)) % GROUPS, 1 - half)
                        k += len(max_share(causal, steps[pos]))
                        if reg_lead(pos):
                            k += QBLOCKS
                        if reg_lead(pos - 1):
                            k += 1
                            wait_apart(sp, item_used, it * BODY + (LEAD + k), passed_sp)
                            sp.dma_start(qr[half][SPLIT_ROWS + 2:SPLIT_ROWS + 4, :, :]
                                         .rearrange("r h q -> r (h q)"),
                                         reg_turned[:, :]).then_inc(reg_rows_in, 16)
                    if pos - LAG - 1 in last_step:
                        u = last_step[pos - LAG - 1]
                        half, i = units[u]
                        k += 1
                        if not causal:
                            wait_apart(sp, item_used, it * BODY + (LEAD + k), passed_sp)
                        n = it * 2 + half
                        if causal:
                            pass
                        elif i == REG_UNIT:
                            sp.dma_start(reg_result[bass.ds(n, 1)].rearrange("o r x -> (o r) x"),
                                         y_sb[0:8, u % 2, 0:HG, :].rearrange("p a d -> p (a d)"))\
                              .then_inc(y_stored[u % 2], 16)
                        else:
                            sp.dma_start(result[bass.ds(n, 1), i].rearrange("o p x -> (o p) x"),
                                         y_sb[:, u % 2, :, :].rearrange("p a d -> p (a d)")).then_inc(y_stored[u % 2], 16)
                    if packed_before(pos):
                        k += 1
                        store_rows(*packed_before(pos), it * BODY + (LEAD + k))
            for s in range(2):
                sp.wait_ge(y_stored[s], 16 * ((0 if causal else 1) + NBODY * NUNIT // 2))
            sp.wait_ge(rows_in, ROWS_DMA * (LEAD_UNITS + NBODY * MAIN))

        @block.gpsimd
        def _(pool):
            for p in range(2):
                nc.gpsimd.memset(kt[p][SPLIT_ROWS:SPLIT_ROWS + 4, :, :], 1.0).then_inc(ones_set, 1)
            if not causal:
                return
            by_group = result.rearrange("(b i) p t (g e) -> i g b p t e", i=QBLOCKS, g=GPB)
            with pool.Fori(0, NBODY) as it:
                k = 0
                for pos in range(NSTEP + LAG + 2):
                    k += len(max_share(causal, steps[pos])) if pos < NSTEP else 0
                    if pos - LAG - 1 in last_step:
                        u = last_step[pos - LAG - 1]
                        half, i = units[u]
                        k += 1
                        wait_apart(pool, item_used, it * BODY + (LEAD + k), passed_pool)
                        b, g = it // 2, (it % 2) * 2 + half
                        pool.dma_start(by_group[i][bass.ds(g, 1), bass.ds(b, 1)]
                                       .rearrange("g b p t e -> (g b p) t e"),
                                       y_sb[:, u % 2, :, :].rearrange("p (t h) d -> p t (h d)", h=HG),
                                       accum_op=ALU.add).then_inc(y_stored[u % 2], 16)
                        wait_apart(pool, y_stored[u % 2], it * (8 * NUNIT) + 16 * (u // 2 + 1), y_free[u % 2])
                    if packed_before(pos):
                        k += 1

        @block.tensor
        def _(pe):
            ident = const["ident"]

            def slot(k):
                return small[(k - LEAD) % 3]

            def max_item(par, i, h, t, kb, k, free):
                if free is not None:
                    pe.wait_ge(item_used, free)
                diag = causal and kb == i
                w = P * (t + 1) if diag else QB
                lhs = qt[par][0:KMAX, h, i * QB + t * P:i * QB + (t + 1) * P]
                mm = nc.tensor.matmul(slot(k)[:, 0:w], lhs, kt[par][0:KMAX, h, kb * QB:kb * QB + w],
                                      start=True, stop=not diag)
                if diag:
                    mm = nc.tensor.matmul(slot(k)[:, w - P:w], const["ident_bf"][:, :], const["mask_max"][:, :],
                                          start=False, stop=True)
                mm.then_inc(item_made, 1)

            def turn_max(k, packs, free):
                pe.wait_ge(max_packed, packs)
                pe.wait_ge(item_used, free)
                nc.tensor.transpose(slot(k)[0:32, 0:P], packed[:, :, :].rearrange("p r a -> p (r a)"),
                                    ident[:, :]).then_inc(item_made, 1)

            pe.wait_ge(ones_set, 2)
            pe.wait_ge(cleared, 1)
            pe.wait_ge(loaded[0], 16 * LOADS)
            k = 0
            for i, h, t, kb, last in lead_blocks:
                max_item(0, i, h, t, kb, k, k - 2 if k >= 3 else None)
                k += 1
                if last:
                    turn_max(k, i + 1, k - 2)
                    k += 1
            with pe.Fori(0, NBODY) as it:
                k, e, main, turns = 0, 0, 0, 0
                for pos in range(NSTEP + LAG + 2):
                    if pos < NSTEP:
                        u, half, i, j = steps[pos]
                        if i == REG_UNIT:
                            pe.wait_ge(reg_rows_in, it * 32 + 16 * (half + 1))
                            for two in range(2):
                                pe.wait_ge(exp_done, it * (2 * NSTEP) + (e - 1))
                                for j8 in range(8):
                                    for h in range(HG):
                                        jj = 8 * two + j8
                                        mm = nc.tensor.matmul(
                                            score[:, e % 2, 0, (j8 * HG + h) * 8:(j8 * HG + h) * 8 + 8],
                                            kt[half][0:KEXP, h, jj * P:(jj + 1) * P], qr[half][0:KEXP, h, 0:8],
                                            start=True, stop=True)
                                mm.then_inc(score_made, 1)
                                e += 1
                        else:
                            blocks = max_share(causal, steps[pos])
                            if j == 0:
                                pe.wait_ge(rows_in, it * (ROWS_DMA * MAIN) + ROWS_DMA * (main + 1))
                                main += 1
                            if blocks[-1][0] != half and (j == 0 or max_share(causal, steps[pos - 1])[-1][0] == half):
                                pe.wait_ge(loaded[1 - half], it * (16 * LOADS) + 16 * LOADS * (1 + half))
                            lo = P * (j - 4 * i) if causal and j >= 4 * i else 0
                            for two in range(2):
                                if e >= 2:
                                    pe.wait_ge(exp_done, it * (2 * NSTEP) + (e - 1))
                                for hh in range(2):
                                    h = 2 * two + hh
                                    diag = causal and j >= 4 * i
                                    mm = nc.tensor.matmul(score[:, e % 2, hh, lo:QB],
                                                          kt[half][0:KEXP, h, j * P:(j + 1) * P],
                                                          qt[half][0:KEXP, h, i * QB + lo:(i + 1) * QB],
                                                          start=True, stop=not diag)
                                    if diag:
                                        mm = nc.tensor.matmul(score[:, e % 2, hh, lo:lo + P],
                                                              const["ident_bf"][:, :], const["mask_exp"][:, :],
                                                              start=False, stop=True)
                                    if hh == 1:
                                        mm.then_inc(score_made, 1)
                                        e += 1
                                    for ahead, ai, ah, t, kb, _ in blocks[len(blocks) * h // HG:
                                                                          len(blocks) * (h + 1) // HG]:
                                        max_item(ahead, ai, ah, t, kb, LEAD + k, it * BODY + (LEAD + k - 2))
                                        k += 1
                        if reg_lead(pos):
                            for kb in range(QBLOCKS):
                                pe.wait_ge(item_used, it * BODY + (LEAD + k - 2))
                                for h in range(HG):
                                    mm = nc.tensor.matmul(slot(LEAD + k)[32 * h:32 * h + 32, :],
                                                          qr[half][0:KMAX, h, :],
                                                          kt[half][0:KMAX, h, kb * QB:(kb + 1) * QB],
                                                          start=True, stop=True)
                                mm.then_inc(item_made, 1)
                                k += 1
                        if reg_lead(pos - 1):
                            pe.wait_ge(reg_max_packed, it * 2 + (half + 1))
                            pe.wait_ge(item_used, it * BODY + (LEAD + k - 2))
                            nc.tensor.transpose(slot(LEAD + k)[0:2, 0:P], reg_packed[:, :], ident[:, :])\
                              .then_inc(item_made, 1)
                            k += 1
                    if 0 <= pos - LAG < NSTEP:
                        s = pos - LAG
                        u, half, i, j = steps[s]
                        pe.wait_ge(exp_done, it * (2 * NSTEP) + 2 * (s + 1))
                        if j == 0 and u > 0:
                            pe.wait_ge(o_copied, it * NUNIT + u)
                        if i == REG_UNIT:
                            for jj in range(KTILES):
                                for h in range(HG):
                                    c = ((jj % 8) * HG + h) * 8
                                    mm = nc.tensor.matmul(o_ps[32 * h:32 * h + VW, 0:8], vt[half][:, jj, h, :],
                                                          prob[:, s % PRING, jj // 8, c:c + 8],
                                                          start=(jj == 0), stop=(jj == KTILES - 1))
                        else:
                            lo = P * (j - 4 * i) if causal and j >= 4 * i else 0
                            for h in range(HG):
                                mm = nc.tensor.matmul(o_ps[32 * h:32 * h + VW, lo:QB], vt[half][:, j, h, :],
                                                      prob[:, s % PRING, h, lo:QB],
                                                      start=(j == 0), stop=(s in last_step))
                        mm.then_inc(pv_done, 1)
                    if pos - LAG - 1 in last_step:
                        u = last_step[pos - LAG - 1]
                        pe.wait_ge(o_copied, it * NUNIT + (u + 1))
                        pe.wait_ge(item_used, it * BODY + (LEAD + k - 2))
                        if units[u][1] == REG_UNIT:
                            mm = nc.tensor.transpose(slot(LEAD + k)[0:8, 0:P], o_sb[:, u % 2, 0:8], ident[:, :])
                        else:
                            for t in range(4):
                                mm = nc.tensor.transpose(slot(LEAD + k)[:, t * P:(t + 1) * P],
                                                         o_sb[:, u % 2, t * P:(t + 1) * P], ident[:, :])
                        mm.then_inc(item_made, 1)
                        k += 1
                    if packed_before(pos):
                        turns += 1
                        turn_max(LEAD + k, it * MAIN + (LEAD_UNITS + turns), it * BODY + (LEAD + k - 2))
                        k += 1
                assert k == BODY and e == 2 * NSTEP and main == MAIN

        @block.scalar
        def _(act):
            with act.Fori(0, NBODY) as it:
                e = 0
                for pos in range(NSTEP + LAG + 2):
                    if pos < NSTEP:
                        u, half, i, j = steps[pos]
                        lo = P * (j - 4 * i) if causal and j >= 4 * i else 0
                        if pos >= PRING:
                            act.wait_ge(pv_done, it * NSTEP + (pos - PRING + 1))
                        for two in range(2):
                            act.wait_ge(score_made, it * (2 * NSTEP) + (e + 1))
                            if i == REG_UNIT:
                                nc.scalar.activation(prob[:, pos % PRING, two, 0:256], score[:, e % 2, 0, 0:256],
                                                     ACT.Exp, scale=SCALE).then_inc(exp_done, 1)
                            else:
                                nc.scalar.activation(prob[:, pos % PRING, 2 * two:2 * two + 2, lo:QB],
                                                     score[:, e % 2, :, lo:QB], ACT.Exp,
                                                     scale=SCALE).then_inc(exp_done, 1)
                            e += 1
                    if pos - LAG in last_step:
                        u = last_step[pos - LAG]
                        w = 8 if units[u][1] == REG_UNIT else QB
                        act.wait_ge(pv_done, it * NSTEP + (pos - LAG + 1))
                        nc.scalar.copy(o_sb[:, u % 2, 0:w], o_ps[:, 0:w]).then_inc(o_copied, 1)

        @block.vector
        def _(dve):
            nc.vector.memset(o_ps[:, :], 0.0).then_inc(cleared, 1)
            for s in range(2):
                if causal:
                    dve.sem_inc(y_free[s], 1)
                else:
                    dve.sem_inc(y_stored[s], 16)

            def reduce_item(k, i, h, t, kb, made):
                dve.wait_ge(item_made, made)
                w = P * (t + 1) if causal and kb == i else QB
                nc.vector.tensor_reduce(part_max[:, 4 * h + t, kb:kb + 1], small[(k - LEAD) % 3][:, 0:w], AX.X,
                                        ALU.max).then_inc(item_used, 1)

            def pack(parts_ap, minus, high, out_ap, reduced, step, packed_sem):
                dve.wait_ge(item_used, reduced)
                nc.vector.tensor_reduce(minus, parts_ap, AX.X, ALU.max, negate=True).then_inc(step_done, 1)
                dve.wait_ge(step_done, step)
                nc.vector.tensor_copy(high, minus).then_inc(step_done, 1)
                dve.wait_ge(step_done, step + 1)
                nc.vector.tensor_copy(out_ap[0], high)
                nc.vector.tensor_tensor(out_ap[1], minus, high, ALU.subtract).then_inc(packed_sem, 1)

            def turned_out(k, made, rows):
                dve.wait_ge(item_made, made)
                if rows is not None:
                    dve.wait_ge(rows_in, rows)
                nc.vector.tensor_copy(turned[:, :], small[(k - LEAD) % 3][0:32, 0:P]).then_inc(item_used, 1)

            def pack_unit(i, reduced, step):
                pack(part_max[:, :, 0:i + 1] if causal else part_max[:, :, :], minus_max[:, :], high_max[:, :],
                     (packed[:, 0, :], packed[:, 1, :]), reduced, step, max_packed)

            k = 0
            for i, h, t, kb, last in lead_blocks:
                reduce_item(k, i, h, t, kb, k + 1)
                k += 1
                if last:
                    pack_unit(i, k, M_STEPS * i + 1)
                    turned_out(k, k + 1, ROWS_DMA * i if i else None)
                    k += 1
            with dve.Fori(0, NBODY) as it:
                k, c, turns = 0, 0, 0
                for pos in range(NSTEP + LAG + 2):
                    if pos < NSTEP:
                        for _, i, h, t, kb, last in max_share(causal, steps[pos]):
                            reduce_item(LEAD + k, i, h, t, kb, it * BODY + (LEAD + k + 1))
                            k += 1
                            if last:
                                pack_unit(i, it * BODY + (LEAD + k), it * BODY_STEPS + (LEAD_STEPS + c + 1))
                                c += M_STEPS
                        if reg_lead(pos):
                            for kb in range(QBLOCKS):
                                dve.wait_ge(item_made, it * BODY + (LEAD + k + 1))
                                nc.vector.tensor_reduce(reg_part[:, kb:kb + 1], small[k % 3][:, :], AX.X,
                                                        ALU.max).then_inc(item_used, 1)
                                k += 1
                            pack(reg_part[:, :], reg_minus[:, :], reg_high[:, :],
                                 (reg_packed[:, 0:1], reg_packed[:, 1:2]),
                                 it * BODY + (LEAD + k), it * BODY_STEPS + (LEAD_STEPS + c + 1), reg_max_packed)
                            c += M_STEPS
                        if reg_lead(pos - 1):
                            dve.wait_ge(item_made, it * BODY + (LEAD + k + 1))
                            nc.vector.tensor_copy(reg_turned[:, :], small[k % 3][0:2, 0:P]).then_inc(item_used, 1)
                            k += 1
                    if pos - LAG - 1 in last_step:
                        u = last_step[pos - LAG - 1]
                        dve.wait_ge(item_made, it * BODY + (LEAD + k + 1))
                        reg = units[u][1] == REG_UNIT
                        rows, heads = (8, HG) if reg else (P, 4 * HG)
                        o = small[k % 3][0:rows, 0:32 * heads].rearrange("p (a e) -> p a e", e=32)
                        nc.vector.reciprocal(inv[0:rows, u % 2, 0:heads], o[:, :, D]).then_inc(step_done, 1)
                        c += 1
                        dve.wait_ge(step_done, it * BODY_STEPS + (LEAD_STEPS + c))
                        if causal:
                            dve.wait_ge(y_free[u % 2], it * (NUNIT // 2) + (u // 2 + 1))
                        else:
                            dve.wait_ge(y_stored[u % 2], it * (8 * NUNIT) + 16 * (u // 2 + 1))
                        nc.vector.scalar_tensor_tensor(
                            y_sb[0:rows, u % 2, 0:heads, :], o[:, :, 0:D],
                            const["beta"][0:rows, :] if causal else 1.0,
                            inv[0:rows, u % 2, 0:heads].unsqueeze(2).broadcast_to([rows, heads, D]),
                            ALU.mult, ALU.mult).then_inc(item_used, 1)
                        k += 1
                    if packed_before(pos):
                        turned_out(LEAD + k, it * BODY + (LEAD + k + 1),
                                   it * (ROWS_DMA * MAIN) + ROWS_DMA * (LEAD_UNITS + turns))
                        turns += 1
                        k += 1
                assert k == BODY and c == BODY_STEPS


def refine_rsqrt(dve, sem, at, y, v, t):
    nc_v = dve
    nc_v.tensor_tensor(t, y, y, ALU.mult).then_inc(sem, 1)
    dve.wait_ge(sem, at + 1)
    nc_v.tensor_tensor(t, t, v, ALU.mult).then_inc(sem, 1)
    dve.wait_ge(sem, at + 2)
    nc_v.tensor_scalar(t, t, -0.5, 1.5, ALU.mult, ALU.add).then_inc(sem, 1)
    dve.wait_ge(sem, at + 3)
    nc_v.tensor_tensor(y, y, t, ALU.mult).then_inc(sem, 1)
    dve.wait_ge(sem, at + 4)


def constants(nc, sems, sb, w_attn, alpha, beta, gamma, g_info, w_qkv, w_proj, b_proj):
    c = {
        "ident": sb("ident", [P, P], F32), "ident_bf": sb("ident_bf", [P, P], BF16),
        "mask_max": sb("mask_max", [P, P], BF16), "mask_exp": sb("mask_exp", [P, P], BF16),
        "ones": sb("ones", [P, P], F32), "upto": sb("upto", [P, P], F32),
        "bias": sb("bias", [P, C], F32), "qg": sb("qg", [P, H, D], F32),
        "alpha": sb("alpha", [P, 1], F32), "beta": sb("beta", [P, 1], F32), "gamma": sb("gamma", [P, 1], F32),
        "share": sb("share", [P, KTILES], F32), "eps": sb("eps", [P, 1], F32),
        "w_a": sb("w_a", [P, KC, 2 * C], F32), "w_f": sb("w_f", [P, KC, 3 * C], F32),
        "w_p": sb("w_p", [P, KC, C], F32),
    }
    with ExitStack() as ctx:
        w_rows = ctx.enter_context(nc.sbuf_tensor("w_rows", [P, 4, C], F32))
        sq = ctx.enter_context(nc.sbuf_tensor("sq", [P, H, D], F32))
        n2 = ctx.enter_context(nc.sbuf_tensor("n2", [P, H], F32))
        y = ctx.enter_context(nc.sbuf_tensor("y", [P, H], F32))
        t = ctx.enter_context(nc.sbuf_tensor("t", [P, H], F32))
        turned = ctx.enter_context(nc.psum_tensor("turned_w", [P, KC, 2 * C], F32))
        w_in = sems.enter_context(nc.semaphore("const_w_in"))
        rows_in = sems.enter_context(nc.semaphore("const_rows_in"))
        filled = sems.enter_context(nc.semaphore("const_filled"))
        shaped = sems.enter_context(nc.semaphore("const_shaped"))
        w_turned = sems.enter_context(nc.semaphore("const_w_turned"))
        rooted = sems.enter_context(nc.semaphore("const_rooted"))
        done = sems.enter_context(nc.semaphore("const_steps"))
        block = ctx.enter_context(nc.Block())

        @block.sync
        def _(sp):
            sp.dma_start(w_rows[:, :, :], w_attn.rearrange("(m p) c -> p m c", p=P)).then_inc(w_in, 16)
            sp.dma_start(c["bias"][:, :], b_proj.partition_broadcast(P)).then_inc(rows_in, 16)
            sp.dma_start(c["qg"][:, :, :].rearrange("p h d -> p (h d)"), g_info[0, 0, :].partition_broadcast(P))\
              .then_inc(rows_in, 16)
            for name, ap in (("alpha", alpha), ("beta", beta), ("gamma", gamma)):
                sp.dma_start(c[name][:, :], ap.partition_broadcast(P)).then_inc(rows_in, 16)
            sp.dma_start(c["w_f"][:, :, :], w_qkv.rearrange("(k p) o -> p k o", p=P)).then_inc(rows_in, 16)
            sp.dma_start(c["w_p"][:, :, :], w_proj.rearrange("(k p) o -> p k o", p=P)).then_inc(rows_in, 16)
            sp.wait_ge(rows_in, 16 * 7)

        @block.gpsimd
        def _(pool):
            for name, value in (("ident", 0.0), ("ident_bf", 0.0), ("mask_max", 0.0), ("mask_exp", 0.0),
                                ("upto", 1.0), ("ones", 1.0), ("eps", EPS)):
                nc.gpsimd.memset(c[name][:, :], value).then_inc(filled, 1)
            pool.wait_ge(filled, 7)
            for name, sign, op, fill in (("ident", 1, ALU.not_equal, 1.0), ("ident_bf", 1, ALU.not_equal, 1.0),
                                         ("mask_max", 1, ALU.is_ge, MASKED), ("mask_exp", -1, ALU.is_ge, MASKED),
                                         ("upto", -1, ALU.is_ge, 0.0)):
                nc.gpsimd.affine_select(out=c[name][:, :], in_=c[name][:, :], compare_op=op, fill=fill, base=0,
                                        pattern=[[-sign, P]], channel_multiplier=sign).then_inc(shaped, 1)
            nc.gpsimd.iota(c["share"][:, :], pattern=[[P, KTILES]], base=1, channel_multiplier=1,
                           allow_small_or_imprecise_dtypes=True).then_inc(shaped, 1)

        @block.tensor
        def _(pe):
            pe.wait_ge(w_in, 16)
            pe.wait_ge(shaped, 1)
            for k in range(KC):
                for m in range(4):
                    mm = nc.tensor.transpose(turned[:, k, m * P:(m + 1) * P], w_rows[:, m, k * P:(k + 1) * P],
                                             c["ident"][:, :])
            mm.then_inc(w_turned, 1)

        @block.scalar
        def _(act):
            act.wait_ge(w_turned, 1)
            for k in range(KC):
                nc.scalar.copy(c["w_a"][:, k, :], turned[:, k, :])
            act.wait_ge(done, 2)
            nc.scalar.activation(y[:, :], n2[:, :], ACT.Sqrt).then_inc(rooted, 1)

        @block.vector
        def _(dve):
            dve.wait_ge(rows_in, 16 * 7)
            nc.vector.tensor_tensor(sq[:, :, :], c["qg"][:, :, :], c["qg"][:, :, :], ALU.mult).then_inc(done, 1)
            dve.wait_ge(done, 1)
            nc.vector.tensor_reduce(n2[:, :], sq[:, :, :], AX.X, ALU.add).then_inc(done, 1)
            dve.wait_ge(rooted, 1)
            nc.vector.reciprocal(y[:, :], y[:, :]).then_inc(done, 1)
            dve.wait_ge(done, 3)
            refine_rsqrt(dve, done, 3, y[:, :], n2[:, :], t[:, :])
            nc.vector.tensor_tensor(c["qg"][:, :, :], c["qg"][:, :, :],
                                    y[:, :].unsqueeze(2).broadcast_to([P, H, D]), ALU.mult).then_inc(done, 1)
            dve.wait_ge(shaped, 6)
            nc.vector.reciprocal(c["share"][:, :], c["share"][:, :]).then_inc(done, 1)
            dve.wait_ge(done, 9)
            nc.vector.tensor_scalar(c["share"][:, :], c["share"][:, :], c["gamma"][:, :], -1.0, ALU.mult,
                                    ALU.mult).then_inc(done, 1)
    return c


def prepare(nc, sems, x, parts, values, base_out, dots, norms, const):
    MT = 8
    with ExitStack() as ctx:
        def sb(name, shape, dt=F32):
            return ctx.enter_context(nc.sbuf_tensor(f"prep_{name}", shape, dt))

        def ps(name, shape):
            return ctx.enter_context(nc.psum_tensor(f"prep_{name}", shape, F32))

        def sem(name):
            return sems.enter_context(nc.semaphore(f"prep_{name}"))

        xs = sb("xs", [P, 2, 4, C])
        xn = sb("xn", [P, 2, 4, C])
        stats = sb("stats", [P, 4, 6])
        mv = sb("mv", [P, 4, 2])
        var = sb("var", [P, 4])
        rstd = sb("rstd", [P, 4])
        newton = sb("newton", [P, 4])
        xn_t = sb("xn_t", [P, KC, QB])
        acc = sb("acc", [P, 2, 4, C])
        base = sb("base", [P, 2, 4, C])
        whole = sb("whole", [P, 2, QB])
        rest = sb("rest", [P, 2, QB])
        split = sb("split", [P, 4, 3, QB], BF16)
        qs = sb("qs", [P, 2, H, D])
        prod = sb("prod", [P, 2, H, D])
        square = sb("square", [P, 2, H, D])
        v_a = sb("v_a", [P, 2, GPB, 4, HG, VW])
        v_f = sb("v_f", [P, 2, GPB, 4, HG, VW])
        p_turn = ps("p_turn", [P, KC, QB])
        p_mean = ps("p_mean", [P, 2, 2, C])
        p_proj = ps("p_proj", [P, 2, QB])
        p_qv = ps("p_qv", [P, 2, 2 * C])

        x_in = [sem(f"x_in{p}") for p in range(2)]
        x_free = sem("x_free")
        stat = sem("stat")
        std_asked = sem("std_asked")
        std_made = sem("std_made")
        xn_made = sem("xn_made")
        turn_made = sem("turn_made")
        turn_copied = sem("turn_copied")
        acc_step = sem("acc_step")
        mean_made = sem("mean_made")
        mean_used = sem("mean_used")
        base_begun = sem("base_begun")
        base_step = sem("base_step")
        base_stored = [sem(f"base_stored{p}") for p in range(2)]
        proj_made = sem("proj_made")
        whole_made = sem("whole_made")
        high_made = sem("high_made")
        rest_made = sem("rest_made")
        mid_made = sem("mid_made")
        low_made = sem("low_made")
        split_out = [sem(f"split_out{s}") for s in range(4)]
        qv_made = sem("qv_made")
        q_copied = sem("q_copied")
        v_copied = sem("v_copied")
        sim_step = sem("sim_step")
        sim_done = sem("sim_done")
        v_a_made = sem("v_a_made")
        ones_set = sem("ones_set")
        v_out = [sem(f"v_out{p}") for p in range(2)]

        x_v = x.rearrange("b (c t p) e -> (b c) p t e", p=P, t=4)
        passed_sp = sem("passed_sp")
        passed_pool = sem("passed_pool")
        passed_dve = sem("passed_dve")
        block = ctx.enter_context(nc.Block())

        @block.sync
        def _(sp):
            for p in range(2):
                sp.dma_start(xs[:, p, :, :], x_v[p]).then_inc(x_in[p], 16)
            with sp.Fori(0, B) as b:
                for c in range(4):
                    par, G = c % 2, b * 4 + c
                    wait_apart(sp, x_free, G + 1, passed_sp)
                    sp.dma_start(xs[:, par, :, :], x_v[bass.ds((G + 2) % CHUNKS, 1)]
                                 .rearrange("o p t e -> (o p) t e")).then_inc(x_in[par], 16)
                    for m in range(MT):
                        wait_apart(sp, low_made, b * (4 * MT) + (MT * c + m + 1 + 2), passed_sp)
                        sp.dma_start(parts[m // 2][:, bass.ds(b * C + (m % 2) * P, P), c * QB:(c + 1) * QB]
                                     .rearrange("r p t -> p r t"), split[:, m % 4, :, :])\
                          .then_inc(split_out[m % 4], 16)
                    wait_apart(sp, base_step, b * 20 + (5 * c + 5), passed_sp)
                    sp.dma_start(base_out[bass.ds(G, 1)].rearrange("o p t e -> (o p) t e"),
                                 base[:, par, :, :]).then_inc(base_stored[par], 16)
                    wait_apart(sp, v_a_made, G + 1, passed_sp)
                    wait_apart(sp, v_copied, b * 16 + (4 * c + 4 + 2), passed_sp)
                    for a, v in ((0, v_a), (1, v_f)):
                        sp.dma_start(values[a][bass.ds(b * GPB, GPB), :, 4 * c * HG * VW:4 * (c + 1) * HG * VW]
                                     .rearrange("g p y -> p g y"),
                                     v[:, par, :, :, :, :].rearrange("p g t h e -> p g (t h e)"))\
                          .then_inc(v_out[par], 16)
            for p in range(2):
                sp.wait_ge(x_in[p], 16 * (CHUNKS // 2 + 1))
                sp.wait_ge(base_stored[p], 16 * (CHUNKS // 2 + 1))
                sp.wait_ge(v_out[p], 32 * (CHUNKS // 2 + 1))
            for s in range(4):
                sp.wait_ge(split_out[s], 16 * (2 * CHUNKS + 1))

        @block.tensor
        def _(pe):
            with pe.Fori(0, B) as b:
                for c in range(4):
                    par, G = c % 2, b * 4 + c
                    pe.wait_ge(xn_made, G + 1)
                    for k in range(KC):
                        for t in range(4):
                            mm = nc.tensor.transpose(p_turn[:, k, t * P:(t + 1) * P],
                                                     xn[:, par, t, k * P:(k + 1) * P], const["ident"][:, :])
                    mm.then_inc(turn_made, 1)
                    pe.wait_ge(acc_step, b * 16 + (4 * c + 3 + 1))
                    for two in range(2):
                        pe.wait_ge(mean_used, b * 8 + (2 * c + two + 1))
                        for t in range(2 * two, 2 * two + 2):
                            nc.tensor.matmul(p_mean[:, two, t % 2, :], const["upto"][:, :], xn[:, par, t, :],
                                             start=True, stop=False)
                            mm = nc.tensor.matmul(p_mean[:, two, t % 2, :], const["ones"][:, :], acc[:, par, t, :],
                                                  start=False, stop=True)
                        mm.then_inc(mean_made, 1)
                    pe.wait_ge(turn_copied, b * 8 + (2 * c + 2))
                    for m in range(MT):
                        w = const["w_a" if m < 4 else "w_f"]
                        pe.wait_ge(whole_made, b * (4 * MT) + (MT * c + m + 1))
                        for k in range(KC):
                            mm = nc.tensor.matmul(p_proj[:, m % 2, :], w[:, k, (m % 4) * P:(m % 4 + 1) * P],
                                                  xn_t[:, k, :], start=(k == 0), stop=(k == KC - 1))
                        mm.then_inc(proj_made, 1)
                    w_qv = const["w_f"][:, :, :].rearrange("p k (s o) -> p k s o", o=C)
                    for t in range(4):
                        pe.wait_ge(v_copied, b * 16 + (4 * c + t + 1))
                        for k in range(KC):
                            mm = nc.tensor.matmul(p_qv[:, t % 2, :], xn_t[:, k, t * P:(t + 1) * P],
                                                  w_qv[:, k, 0:3:2, :], start=(k == 0), stop=(k == KC - 1))
                        mm.then_inc(qv_made, 1)

        @block.scalar
        def _(act):
            act.sem_inc(whole_made, 2)
            act.sem_inc(v_copied, 2)

            def root(asked):
                act.wait_ge(std_asked, asked)
                nc.scalar.activation(rstd[:, :], var[:, :], ACT.Sqrt).then_inc(std_made, 1)

            root(1)
            with act.Fori(0, B) as b:
                for c in range(4):
                    par, G = c % 2, b * 4 + c
                    act.wait_ge(turn_made, G + 1)
                    for k in range(KC):
                        nc.scalar.copy(xn_t[:, k, :], p_turn[:, k, :]).then_inc(turn_copied, 1)
                    for m in range(MT):
                        act.wait_ge(proj_made, b * (4 * MT) + (MT * c + m + 1))
                        act.wait_ge(rest_made, b * (4 * MT) + (MT * c + m + 1))
                        nc.scalar.copy(whole[:, m % 2, :], p_proj[:, m % 2, :]).then_inc(whole_made, 1)
                        if m == 4:
                            root(G + 2)
                    act.wait_ge(v_out[par], b * 64 + 32 * (c // 2 + 1))
                    if c == 0:
                        act.wait_ge(ones_set, 2)
                    for t in range(4):
                        act.wait_ge(qv_made, b * 16 + (4 * c + t + 1))
                        act.wait_ge(sim_done, b * 16 + (4 * c + t + 1))
                        nc.scalar.copy(qs[:, t % 2, :, :].rearrange("p h d -> p (h d)"),
                                       p_qv[:, t % 2, 0:C]).then_inc(q_copied, 1)
                        nc.scalar.copy(v_f[:, par, :, t, :, 0:D],
                                       p_qv[:, t % 2, C:2 * C].rearrange("p (g h d) -> p g h d", g=GPB, d=D))\
                          .then_inc(v_copied, 1)

        @block.gpsimd
        def _(pool):
            pool.sem_inc(low_made, 2)
            for v in (v_a, v_f):
                nc.gpsimd.memset(v[:, :, :, :, :, :], 1.0).then_inc(ones_set, 1)
            nc.gpsimd.memset(acc[:, 0, 0, :], 0.0).then_inc(acc_step, 1)
            pool.wait_ge(ones_set, 2)
            with pool.Fori(0, B) as b:
                for c in range(4):
                    par, G = c % 2, b * 4 + c
                    pool.wait_ge(xn_made, G + 1)
                    for t in range(4):
                        wait_apart(pool, acc_step, b * 16 + (4 * c + t + 1), passed_pool)
                        if t < 3 or c < 3:
                            nxt = acc[:, par, t + 1, :] if t < 3 else acc[:, 1 - par, 0, :]
                            nc.gpsimd.tensor_tensor(nxt, acc[:, par, t, :], xn[:, par, t, :], ALU.add)\
                              .then_inc(acc_step, 1)
                        else:
                            nc.gpsimd.memset(acc[:, 0, 0, :], 0.0).then_inc(acc_step, 1)
                    pool.wait_ge(base_stored[par], b * 32 + 16 * (c // 2 + 1))
                    nc.gpsimd.tensor_tensor(base[:, par, :, :], xs[:, par, :, :],
                                            const["bias"][:, :].unsqueeze(1).broadcast_to([P, 4, C]), ALU.add)\
                      .then_inc(base_begun, 1)
                    pool.wait_ge(base_begun, G + 1)
                    pool.sem_inc(x_free, 1)
                    wait_apart(pool, v_out[par], b * 64 + 32 * (c // 2 + 1), passed_pool)
                    for t in range(4):
                        cp = nc.gpsimd.tensor_copy(v_a[:, par, :, t, :, 0:D],
                                                   xn[:, par, t, :].rearrange("p (g h d) -> p g h d", g=GPB, d=D))
                    cp.then_inc(v_a_made, 1)
                    for m in range(MT):
                        pool.wait_ge(mid_made, b * (4 * MT) + (MT * c + m + 1))
                        nc.gpsimd.tensor_tensor(split[:, m % 4, 2, :], rest[:, m % 2, :], split[:, m % 4, 1, :],
                                                ALU.subtract).then_inc(low_made, 1)

        @block.vector
        def _(dve):
            dve.sem_inc(mean_used, 2)
            dve.sem_inc(rest_made, 2)
            dve.sem_inc(sim_done, 2)
            for p in range(2):
                dve.sem_inc(base_stored[p], 16)
                dve.sem_inc(v_out[p], 32)
            for s in range(4):
                dve.sem_inc(split_out[s], 16)
            STAT = 9

            def norm(par, x_there, G, base_stat):
                dve.wait_ge(x_in[par], x_there)
                for t in range(4):
                    bn = nc.vector.bn_stats(stats[:, t, :], xs[:, par, t, :])
                bn.then_inc(stat, 1)
                wait_apart(dve, stat, base_stat + 1, passed_dve)
                for t in range(4):
                    bn = nc.vector.bn_aggr(mv[:, t, :], stats[:, t, :])
                bn.then_inc(stat, 1)
                dve.wait_ge(stat, base_stat + 2)
                nc.vector.tensor_scalar(var[:, :], mv[:, :, 1], EPS, None, ALU.add).then_inc(std_asked, 1)
                dve.wait_ge(std_made, G + 1)
                dve.wait_ge(std_asked, G + 1)
                nc.vector.reciprocal(rstd[:, :], rstd[:, :]).then_inc(stat, 1)
                dve.wait_ge(stat, base_stat + 3)
                refine_rsqrt(dve, stat, base_stat + 3, rstd[:, :], var[:, :], newton[:, :])
                for t in range(4):
                    ts = nc.vector.tensor_scalar(xn[:, par, t, :], xs[:, par, t, :], mv[:, t, 0:1], rstd[:, t:t + 1],
                                                 ALU.subtract, ALU.mult)
                ts.then_inc(xn_made, 1)

            norm(0, 16, 0, 0)
            with dve.Fori(0, B) as b:
                for c in range(4):
                    par, G = c % 2, b * 4 + c
                    dve.wait_ge(base_begun, G + 1)
                    dve.wait_ge(xn_made, G + 1)
                    nc.vector.scalar_tensor_tensor(base[:, par, :, :].rearrange("p t e -> p (t e)"),
                                                   xn[:, par, :, :].rearrange("p t e -> p (t e)"),
                                                   const["alpha"][:, :],
                                                   base[:, par, :, :].rearrange("p t e -> p (t e)"),
                                                   ALU.mult, ALU.add).then_inc(base_step, 1)
                    dve.wait_ge(base_step, b * 20 + (5 * c + 1))
                    for two in range(2):
                        dve.wait_ge(mean_made, b * 8 + (2 * c + two + 1))
                        for t in range(2 * two, 2 * two + 2):
                            st = nc.vector.scalar_tensor_tensor(
                                base[:, par, t, :], p_mean[:, two, t % 2, :], const["share"][:, 4 * c + t:4 * c + t + 1],
                                base[:, par, t, :], ALU.mult, ALU.add).then_inc(base_step, 1)
                        dve.wait_ge(base_step, b * 20 + (5 * c + 2 * two + 3))
                        dve.sem_inc(mean_used, 1)
                    for m in range(MT):
                        i = MT * c + m
                        dve.wait_ge(split_out[m % 4], b * 128 + 16 * (2 * c + m // 4 + 1))
                        dve.wait_ge(whole_made, b * (4 * MT) + (i + 1 + 2))
                        nc.vector.tensor_copy(split[:, m % 4, 0, :], whole[:, m % 2, :]).then_inc(high_made, 1)
                        dve.wait_ge(high_made, b * (4 * MT) + (i + 1))
                        dve.wait_ge(low_made, b * (4 * MT) + (i + 1))
                        nc.vector.tensor_tensor(rest[:, m % 2, :], whole[:, m % 2, :], split[:, m % 4, 0, :],
                                                ALU.subtract).then_inc(rest_made, 1)
                        dve.wait_ge(rest_made, b * (4 * MT) + (i + 1 + 2))
                        nc.vector.tensor_copy(split[:, m % 4, 1, :], rest[:, m % 2, :]).then_inc(mid_made, 1)
                        if m == 4:
                            norm(1 - par, b * 32 + 16 * ((c + 1) // 2 + 1), G + 1, b * (4 * 7) + 7 * (c + 1))
                    for t in range(4):
                        i = 4 * c + t
                        dve.wait_ge(q_copied, b * 16 + (i + 1))
                        nc.vector.tensor_tensor(prod[:, t % 2, :, :], qs[:, t % 2, :, :], const["qg"][:, :, :],
                                                ALU.mult).then_inc(sim_step, 1)
                        nc.vector.tensor_tensor(square[:, t % 2, :, :], qs[:, t % 2, :, :], qs[:, t % 2, :, :],
                                                ALU.mult).then_inc(sim_step, 1)
                        dve.wait_ge(sim_step, b * 32 + (2 * i + 2))
                        nc.vector.tensor_reduce(dots[:, bass.ds(b * KTILES + i, 1), :]
                                                .rearrange("p o h -> p (o h)"), prod[:, t % 2, :, :], AX.X, ALU.add)
                        nc.vector.tensor_reduce(norms[:, bass.ds(b * KTILES + i, 1), :]
                                                .rearrange("p o h -> p (o h)"), square[:, t % 2, :, :], AX.X,
                                                ALU.add).then_inc(sim_done, 1)


def classify(nc, sems, dots, norms, masks, reg_rows, const):
    NT = B * KTILES
    with ExitStack() as ctx:
        def sb(name, shape, dt=F32):
            return ctx.enter_context(nc.sbuf_tensor(f"class_{name}", shape, dt))

        root = sb("root", [P, NT, H])
        newton = sb("newton", [P, NT, H])
        sim = sb("sim", [P, NT])
        edge = sb("edge", [P, 2, NT])
        ends = sb("ends", [P, 2])
        both = sb("both", [P, 2])
        width = sb("width", [P, 1])
        pos = sb("pos", [P, NT])
        rows = sb("rows", [P, 4, NT])
        rows_t = sb("rows_t", [P, 2, P], BF16)
        reg = sb("reg", [2, P], BF16)
        p_rows = ctx.enter_context(nc.psum_tensor("p_rows", [P, 2, P], F32))
        rooted = sems.enter_context(nc.semaphore("class_rooted"))
        step = sems.enter_context(nc.semaphore("class_step"))
        ends_made = sems.enter_context(nc.semaphore("class_ends_made"))
        ends_shared = sems.enter_context(nc.semaphore("class_ends_shared"))
        rows_made = sems.enter_context(nc.semaphore("class_rows_made"))
        rows_turned = sems.enter_context(nc.semaphore("class_rows_turned"))
        rows_ready = sems.enter_context(nc.semaphore("class_rows_ready"))
        stored = sems.enter_context(nc.semaphore("class_stored"))
        block = ctx.enter_context(nc.Block())

        @block.scalar
        def _(act):
            nc.scalar.activation(root[:, :, :], norms[:, :, :], ACT.Sqrt).then_inc(rooted, 1)

        @block.gpsimd
        def _(pool):
            pool.wait_ge(ends_made, 1)
            nc.gpsimd.partition_all_reduce(both[:, :], ends[:, :], P, bass.bass_isa.ReduceOp.max)\
              .then_inc(ends_shared, 1)

        @block.tensor
        def _(pe):
            pe.wait_ge(rows_made, 1)
            for a in range(2):
                mm = nc.tensor.transpose(p_rows[:, a, :], rows[:, 2 * a:2 * a + 2, :].rearrange("p k t -> p (k t)"),
                                         const["ident"][:, :])
            mm.then_inc(rows_turned, 1)

        @block.sync
        def _(sp):
            sp.wait_ge(rows_ready, 1)
            for k in range(4):
                sp.dma_start(masks[k].rearrange("b (t x) -> (b t) x", x=P),
                             rows_t[64 * (k % 2):64 * (k % 2) + 64, k // 2, :]).then_inc(stored, 16)
            sp.dma_start(reg_rows, reg[:, :]).then_inc(stored, 16)
            sp.wait_ge(stored, 16 * 5)

        @block.vector
        def _(dve):
            count = [0]

            def link(ins):
                ins.then_inc(step, 1)
                count[0] += 1
                dve.wait_ge(step, count[0])

            link(nc.vector.memset(reg[:, :], 0.0))
            link(nc.vector.memset(reg[0:1, :], MASKED))
            dve.wait_ge(rooted, 1)
            link(nc.vector.reciprocal(root[:, :, :], root[:, :, :]))
            refine_rsqrt(dve, step, count[0], root[:, :, :], norms[:, :, :], newton[:, :, :])
            count[0] += 4
            link(nc.vector.tensor_tensor(root[:, :, :], root[:, :, :], dots[:, :, :], ALU.mult))
            link(nc.vector.tensor_reduce(sim[:, :], root[:, :, :], AX.X, ALU.add))
            link(nc.vector.tensor_scalar(sim[:, :], sim[:, :], 1.0 / H, None, ALU.mult))
            nc.vector.tensor_copy(edge[:, 0, :], sim[:, :])
            link(nc.vector.tensor_scalar(edge[:, 1, :], sim[:, :], -1.0, None, ALU.mult))
            link(nc.vector.memset(edge[0:REG, :, 0:NT:KTILES], -3e38))
            nc.vector.tensor_reduce(ends[:, :], edge[:, :, :], AX.X, ALU.max).then_inc(ends_made, 1)
            dve.wait_ge(ends_shared, 1)
            link(nc.vector.tensor_tensor(width[:, :], both[:, 0:1], both[:, 1:2], ALU.add))
            link(nc.vector.reciprocal(width[:, :], width[:, :]))
            link(nc.vector.tensor_scalar(sim[:, :], sim[:, :], both[:, 1:2], width[:, :], ALU.add, ALU.mult))
            link(nc.vector.tensor_scalar(pos[:, :], sim[:, :], 0.9, None, ALU.is_gt))
            nc.vector.tensor_copy(rows[:, 0, :], pos[:, :])
            link(nc.vector.tensor_scalar(rows[:, 1, :], pos[:, :], -1.0, 1.0, ALU.mult, ALU.add))
            link(nc.vector.memset(rows[0:REG, 0:2, 0:NT:KTILES], 0.0))
            link(nc.vector.memset(pos[0:REG, 0:NT:KTILES], 1.0))
            nc.vector.tensor_scalar(rows[:, 2, :], pos[:, :], -MASKED, MASKED, ALU.mult, ALU.add)
            nc.vector.tensor_scalar(rows[:, 3, :], pos[:, :], MASKED, None, ALU.mult).then_inc(rows_made, 1)
            dve.wait_ge(rows_turned, 1)
            nc.vector.tensor_copy(rows_t[:, :, :], p_rows[:, :, :]).then_inc(rows_ready, 1)


def finish(nc, sems, base_in, y_f, y_reg, out, const):
    CAME = 16 * (1 + GPB)
    BUFS = QBLOCKS
    AHEAD = BUFS - 1
    with ExitStack() as ctx:
        def sb(name, shape):
            return ctx.enter_context(nc.sbuf_tensor(f"fin_{name}", shape, F32))

        def sem(name):
            return sems.enter_context(nc.semaphore(f"fin_{name}"))

        yf = sb("yf", [P, BUFS, 4, GPB, HG * D])
        yr = sb("yr", [8, B, GPB, HG * D])
        base = sb("base", [P, BUFS, 4, C])
        yt = sb("yt", [P, 2, KC, QB])
        res = sb("res", [P, BUFS, 4, C])
        p_turn = ctx.enter_context(nc.psum_tensor("fin_turn", [P, 2, KC, QB], F32))
        p_out = ctx.enter_context(nc.psum_tensor("fin_out", [P, 2, 2, C], F32))
        came = [sem(f"came{p}") for p in range(BUFS)]
        reg_came = sem("reg_came")
        reg_step = sem("reg_step")
        turned = sem("turned")
        copied = sem("copied")
        made = sem("made")
        summed = sem("summed")
        stored = [sem(f"stored{p}") for p in range(BUFS)]
        out_v = out.rearrange("b (c t p) e -> (b c) p t e", p=P, t=4)
        passed_sp = sem("passed_sp")
        block = ctx.enter_context(nc.Block())

        @block.sync
        def _(sp):
            def load(n, par, b, c):
                for g in range(GPB):
                    sp.dma_start(yf[:, par, :, g, :], y_f[bass.ds(b * GPB + g, 1), c]
                                 .rearrange("o p (t e) -> (o p) t e", t=4)).then_inc(came[par], 16)
                sp.dma_start(base[:, par, :, :], base_in[bass.ds(n, 1)].rearrange("o p t e -> (o p) t e"))\
                  .then_inc(came[par], 16)

            sp.dma_start(yr[:, :, :, :].rearrange("r b g x -> r (b g) x"), y_reg.rearrange("n r x -> r n x"))\
              .then_inc(reg_came, 16)
            for c in range(AHEAD):
                load(c, c, 0, c)
            with sp.Fori(0, B) as b:
                for c in range(4):
                    G = b * 4 + c
                    wait_apart(sp, summed, b * 8 + (2 * c + 2), passed_sp)
                    load((G + AHEAD) % CHUNKS, (c + AHEAD) % BUFS, b if c == 0 else (b + 1) % B, (c + AHEAD) % BUFS)
                    wait_apart(sp, summed, b * 8 + (2 * c + 2 + 2), passed_sp)
                    sp.dma_start(out_v[bass.ds(G, 1)].rearrange("o p t e -> (o p) t e"), res[:, c, :, :])\
                      .then_inc(stored[c], 16)
            for p in range(BUFS):
                sp.wait_ge(came[p], CAME * (B + (p < AHEAD)))
                sp.wait_ge(stored[p], 16 * (B + 1))

        @block.tensor
        def _(pe):
            with pe.Fori(0, B) as b:
                for c in range(4):
                    pe.wait_ge(came[c], b * CAME + CAME)
                    if c == 0:
                        pe.wait_ge(reg_step, b * 2 + 2)
                    for k in range(KC):
                        for t in range(4):
                            mm = nc.tensor.transpose(p_turn[:, c % 2, k, t * P:(t + 1) * P],
                                                     yf[:, c, t, 2 * k:2 * k + 2, :].rearrange("p g e -> p (g e)"),
                                                     const["ident"][:, :])
                        mm.then_inc(turned, 1)
                    pe.wait_ge(copied, b * 8 + (2 * c + 2))
                    for two in range(2):
                        pe.wait_ge(summed, b * 8 + (2 * c + two + 1))
                        for t in range(2 * two, 2 * two + 2):
                            for k in range(KC):
                                mm = nc.tensor.matmul(p_out[:, two, t % 2, :], yt[:, c % 2, k, t * P:(t + 1) * P],
                                                      const["w_p"][:, k, :], start=(k == 0), stop=(k == KC - 1))
                        mm.then_inc(made, 1)

        @block.scalar
        def _(act):
            with act.Fori(0, B) as b:
                for c in range(4):
                    for k in range(KC):
                        act.wait_ge(turned, b * 8 + (2 * c + k + 1))
                        nc.scalar.copy(yt[:, c % 2, k, :], p_turn[:, c % 2, k, :]).then_inc(copied, 1)

        @block.vector
        def _(dve):
            dve.sem_inc(summed, 2)
            for p in range(BUFS):
                dve.sem_inc(stored[p], 16)
            dve.wait_ge(reg_came, 16)
            with dve.Fori(0, B) as b:
                for c in range(4):
                    if c == 0:
                        dve.wait_ge(came[c], b * CAME + CAME)
                        nc.vector.tensor_tensor(yf[0:REG, c, 0, :, :], yf[0:REG, c, 0, :, :],
                                                yr[0:REG, bass.ds(b, 1), :, :].rearrange("r o g x -> r (o g) x"),
                                                ALU.add).then_inc(reg_step, 1)
                        dve.wait_ge(reg_step, b * 2 + 1)
                        nc.vector.tensor_scalar(yf[0:REG, c, 0, :, :], yf[0:REG, c, 0, :, :], 0.5, None,
                                                ALU.mult).then_inc(reg_step, 1)
                    dve.wait_ge(stored[c], b * 16 + 16)
                    for two in range(2):
                        dve.wait_ge(made, b * 8 + (2 * c + two + 1))
                        nc.vector.tensor_tensor(res[:, c, 2 * two:2 * two + 2, :], p_out[:, two, :, :],
                                                base[:, c, 2 * two:2 * two + 2, :], ALU.add).then_inc(summed, 1)


def build(nc, x, w_attn, alpha, beta, gamma, g_info, w_qkv, w_proj, b_proj, out):
    def dram(name, shape, dt=F32):
        return nc.dram_tensor(name, shape, dt, kind="Internal").ap()

    parts = dram("parts", (4, 3, B * C, T), BF16)
    values = dram("values", (2, GROUPS, P, KTILES * HG * VW))
    base = dram("base", (CHUNKS, P, 4, C))
    masks = dram("masks", (4, B, T), BF16)
    reg_rows = dram("reg_rows", (2, P), BF16)
    y_f = dram("y_f", (GROUPS, QBLOCKS, P, 4 * HG * D))
    y_reg = dram("y_reg", (GROUPS, 8, HG * D))
    with ExitStack() as ctx:
        def sb(name, shape, dt):
            return ctx.enter_context(nc.sbuf_tensor(name, shape, dt))

        const = constants(nc, ctx, sb, w_attn, alpha, beta, gamma, g_info, w_qkv, w_proj, b_proj)
        with ExitStack() as sims:
            dots = sims.enter_context(nc.sbuf_tensor("dots", [P, B * KTILES, H], F32))
            norms = sims.enter_context(nc.sbuf_tensor("norms", [P, B * KTILES, H], F32))
            prepare(nc, ctx, x, parts, values, base, dots, norms, const)
            classify(nc, ctx, dots, norms, masks, reg_rows, const)
        attend(nc, ctx, True, (parts[0], parts[1]), values[0], None, None, base, None, const)
        attend(nc, ctx, False, (parts[2], parts[3]), values[1], masks, reg_rows, y_f, y_reg, const)
        finish(nc, ctx, base, y_f, y_reg, out, const)


_INS = ["L0_attn_x", "L0_attn_W_attn", "L0_attn_alpha", "L0_attn_beta", "L0_attn_gamma", "L0_ffn_g_info",
        "L0_ffn_W_qkv", "L0_ffn_W_proj", "L0_ffn_b_proj"]


def kernel(**inputs):
    import concourse.bacc as _bacc
    from concourse.bass_utils import run_bass_kernel_spmd as _run

    nc = _bacc.Bacc("TRN2", target_bir_lowering=False, num_devices=1)
    arrays, args = {}, []
    for name in _INS:
        a = np.ascontiguousarray(inputs[name])
        arrays[f"in_{name}"] = a
        args.append(nc.dram_tensor(f"in_{name}", a.shape, mybir.dt.from_np(a.dtype), kind="ExternalInput").ap())
    out = nc.dram_tensor("out_0", (B, T, C), F32, kind="ExternalOutput").ap()
    build(nc, *args, out)
    return _run(nc, [arrays], core_ids=[0]).results[0]["out_0"]
```

```python
from contextlib import ExitStack

import numpy as np

import concourse.bass as bass
from concourse import mybir

F32 = mybir.dt.float32
BF16 = mybir.dt.bfloat16
ALU = mybir.AluOpType
ACT = mybir.ActivationFunctionType
AX = mybir.AxisListType

P = 128
B, T, C = 4, 2048, 256
H = 16
D = C // H
REG = 5
HG = 4
GROUPS = B * H // HG
GPB = H // HG
QB = 512
QBLOCKS = T // QB
KTILES = T // P
CHUNKS = B * QBLOCKS
KC = C // P
VW = D + 1
SPLIT_ROWS = 6 * D
Q_PART = (0, 0, 1, 0, 1, 2)
K_PART = (0, 1, 0, 2, 1, 0)
SCALE = float(D) ** -0.5
MASKED = -(2.0 ** 40)
EPS = 1e-5
LAG = 2
PRING = 4
MAX_AHEAD = 96
REG_UNIT = -1
CAUSAL, CLASS = 0, 1
LOADS = (6 * 2 + 1, 6 * 2 + 1 + 8 + 6 + 1)


def wait_apart(engine, sem, value, passed):
    engine.wait_ge(sem, value)
    engine.sem_inc(passed, 1)


def attend_plan():
    units, steps, last_step = [], [], {}
    for half in (CAUSAL, CLASS):
        for i in list(range(QBLOCKS)) + ([] if half == CAUSAL else [REG_UNIT]):
            units.append((half, i))
            n = 1 if i == REG_UNIT else (4 * (i + 1) if half == CAUSAL else KTILES)
            for j in range(n):
                steps.append((len(units) - 1, half, i, j))
            last_step[len(steps) - 1] = len(units) - 1
    return units, steps, last_step


def max_stream():
    out = []
    for half in (CAUSAL, CLASS):
        for i in range(QBLOCKS):
            blocks = [(h, t, kb) for h in range(HG) for t in range(4)
                      for kb in range((i + 1) if half == CAUSAL else QBLOCKS)]
            out += [(half, i, *blk, n == len(blocks) - 1) for n, blk in enumerate(blocks)]
    return out


def max_share(steps, stream, pos):
    if steps[pos][2] == REG_UNIT:
        return []
    per_step = len(stream) // sum(i != REG_UNIT for _, _, i, _ in steps)
    return [stream[n % len(stream)] for n in range(MAX_AHEAD + per_step * pos, MAX_AHEAD + per_step * (pos + 1))]


def load(sp, ops, n, par, parts, values, masks, reg_rows):
    kt, qt, qr, vt, loaded = (ops[name] for name in ("kt", "qt", "qr", "vt", "loaded"))
    q_parts, k_parts = parts[2 * par], parts[2 * par + 1]
    rows = bass.ds(n * HG * D, HG * D)
    for r in range(6):
        for dst, part in ((kt[par], k_parts[K_PART[r]]), (qt[par], q_parts[Q_PART[r]])):
            sp.dma_start(dst[r * D:(r + 1) * D, :, :],
                         part[rows, :].rearrange("(h d) t -> d h t", d=D)).then_inc(loaded[par], 16)
        if par == CLASS:
            sp.dma_start(qr[r * D:(r + 1) * D, :, :],
                         q_parts[Q_PART[r]][rows, 0:32].rearrange("(h d) t -> d h t", d=D))\
              .then_inc(loaded[par], 16)
    sp.dma_start(vt[par][:, :, :, :].rearrange("p k h e -> p (k h e)"),
                 values[par][bass.ds(n, 1)].rearrange("o p x -> (o p) x")).then_inc(loaded[par], 16)
    if par == CLASS:
        for h in range(HG):
            b = n // 4
            sp.dma_start(kt[par][SPLIT_ROWS:SPLIT_ROWS + 2, h, :],
                         masks[0:2, bass.ds(b, 1), :].rearrange("k o t -> k (o t)"))\
              .then_inc(loaded[par], 16)
            sp.dma_start(qt[par][SPLIT_ROWS:SPLIT_ROWS + 2, h, :],
                         masks[2:4, bass.ds(b, 1), :].rearrange("k o t -> k (o t)"))\
              .then_inc(loaded[par], 16)
        sp.dma_start(qr[SPLIT_ROWS:SPLIT_ROWS + 2, :, :].rearrange("r h q -> r (h q)"),
                     reg_rows).then_inc(loaded[par], 16)


def operands(nc, ctx):
    def sb(name, shape, dt=BF16):
        return ctx.enter_context(nc.sbuf_tensor(f"ops_{name}", shape, dt))

    return {
        "kt": [sb(f"kt{p}", [SPLIT_ROWS + 4, HG, T]) for p in range(2)],
        "qt": [sb(f"qt{p}", [SPLIT_ROWS + 4, HG, T]) for p in range(2)],
        "qr": sb("qr", [SPLIT_ROWS + 4, HG, 32]),
        "vt": [sb(f"vt{p}", [P, KTILES, HG, VW], F32) for p in range(2)],
        "loaded": [ctx.enter_context(nc.semaphore(f"ops_loaded{p}")) for p in range(2)],
        "ones_set": ctx.enter_context(nc.semaphore("ops_ones_set")),
    }


def attend(nc, sems, ops, parts, values, masks, reg_rows, base, y_f, y_reg, const):
    units, steps, last_step = attend_plan()
    stream = max_stream()
    NSTEP, NUNIT = len(steps), len(units)
    MAIN = sum(i != REG_UNIT for _, i in units)
    MROW = (SPLIT_ROWS, SPLIT_ROWS + 2)
    KMAX, KEXP = MROW, (SPLIT_ROWS + 2, SPLIT_ROWS + 4)
    lead_blocks = stream[:MAX_AHEAD]
    LEAD_UNITS = sum(last for *_, last in lead_blocks)
    LEAD = MAX_AHEAD + LEAD_UNITS
    BODY = len(stream) + MAIN + NUNIT + QBLOCKS + 1
    assert BODY % 3 == 0
    M_STEPS = 2
    LEAD_STEPS = LEAD_UNITS * M_STEPS
    BODY_STEPS = MAIN * M_STEPS + M_STEPS + NUNIT
    ROWS_DMA = 16 * 2 * HG

    def share(pos):
        return max_share(steps, stream, pos)

    with ExitStack() as ctx:
        def sb(name, shape, dt):
            return ctx.enter_context(nc.sbuf_tensor(f"att_{name}", shape, dt))

        def ps(name, shape, dt):
            return ctx.enter_context(nc.psum_tensor(f"att_{name}", shape, dt))

        def sem(name):
            return sems.enter_context(nc.semaphore(f"att_{name}"))

        kt, qt, qr, vt, loaded = (ops[name] for name in ("kt", "qt", "qr", "vt", "loaded"))
        prob = sb("prob", [P, PRING, HG, QB], F32)
        o_sb = sb("o_sb", [P, 3, QB], F32)
        y_sb = sb("y_sb", [P, NUNIT, 4 * HG, D], F32)
        part_max = sb("part_max", [P, 16, QBLOCKS], F32)
        minus_max = sb("minus_max", [P, 16], F32)
        high_max = sb("high_max", [P, 16], BF16)
        packed = sb("packed", [P, 2, 16], F32)
        turned = sb("turned", [32, P], BF16)
        reg_part = sb("reg_part", [P, QBLOCKS], F32)
        reg_minus = sb("reg_minus", [P, 1], F32)
        reg_high = sb("reg_high", [P, 1], BF16)
        reg_packed = sb("reg_packed", [P, 2], F32)
        reg_turned = sb("reg_turned", [2, P], BF16)
        inv = sb("inv", [P, 2, 16], F32)
        small = [ps(f"small{s}", [P, QB], F32) for s in range(3)]
        score = ps("score", [P, 2, 2, QB], F32)
        o_ps = ps("o_ps", [P, QB], F32)

        cleared = sem("cleared")
        item_made = sem("item_made")
        item_used = sem("item_used")
        step_done = sem("step_done")
        max_packed = sem("max_packed")
        reg_max_packed = sem("reg_max_packed")
        rows_in = sem("rows_in")
        reg_rows_in = sem("reg_rows_in")
        score_made = sem("score_made")
        exp_done = sem("exp_done")
        pv_done = sem("pv_done")
        o_copied = sem("o_copied")
        added = sem("added")
        added_free = sem("added_free")
        y_stored = [sem(f"y_stored{i}") for i in range(QBLOCKS + 1)]

        passed_sp = sem("passed_sp")
        passed_pool = sem("passed_pool")
        block = ctx.enter_context(nc.Block())

        def reg_lead(pos):
            return pos < NSTEP and steps[pos][1:] == (CLASS, 0, 1)

        def packed_before(pos):
            done = [(half, i) for half, i, *_, last in share(pos - 1) if last] if 0 < pos <= NSTEP else []
            return done[0] if done else None

        @block.sync
        def _(sp):
            def store_rows(par, i, used):
                sp.wait_ge(item_used, used)
                for r in range(2):
                    for h in range(HG):
                        sp.dma_start(qt[par][MROW[par] + r:MROW[par] + r + 1, h, i * QB:(i + 1) * QB],
                                     turned[16 * r + 4 * h:16 * r + 4 * h + 4, :]).then_inc(rows_in, 16)

            k = 0
            for half, i, *_, last in lead_blocks:
                k += 1
                if last:
                    k += 1
                    store_rows(half, i, k)
            with sp.Fori(0, GROUPS) as it:
                k = 0
                for pos in range(NSTEP + LAG + 2):
                    if pos < NSTEP:
                        u, half, i, j = steps[pos]
                        if i == 1 and j == 0:
                            wait_apart(sp, pv_done, it * NSTEP + pos, passed_sp)
                            load(sp, ops, (it + half) % GROUPS, 1 - half, parts, values, masks, reg_rows)
                        k += len(share(pos))
                        if reg_lead(pos):
                            k += QBLOCKS
                        if reg_lead(pos - 1):
                            k += 1
                            wait_apart(sp, item_used, it * BODY + (LEAD + k), passed_sp)
                            sp.dma_start(qr[SPLIT_ROWS + 2:SPLIT_ROWS + 4, :, :]
                                         .rearrange("r h q -> r (h q)"),
                                         reg_turned[:, :]).then_inc(reg_rows_in, 16)
                    if pos - LAG - 1 in last_step:
                        u = last_step[pos - LAG - 1]
                        half, i = units[u]
                        k += 1
                        if half == CLASS:
                            wait_apart(sp, item_used, it * BODY + (LEAD + k), passed_sp)
                            if i == REG_UNIT:
                                dst, src = y_reg[bass.ds(it, 1)], y_sb[0:8, u, 0:HG, :]
                            else:
                                dst, src = y_f[bass.ds(it, 1), i], y_sb[:, u, :, :]
                            sp.dma_start(dst.rearrange("o p x -> (o p) x"), src.rearrange("p a d -> p (a d)"))\
                              .then_inc(y_stored[i], 16)
                    if packed_before(pos):
                        k += 1
                        store_rows(*packed_before(pos), it * BODY + (LEAD + k))
            for stored in y_stored:
                sp.wait_ge(stored, 16 * (GROUPS + 1))
            sp.wait_ge(added, 16 * QBLOCKS * GROUPS)
            sp.wait_ge(rows_in, ROWS_DMA * (LEAD_UNITS + GROUPS * MAIN))

        @block.gpsimd
        def _(pool):
            by_group = base.rearrange("(b i) p t (g e) -> i g b p t e", i=QBLOCKS, g=GPB)
            with pool.Fori(0, GROUPS) as it:
                k = 0
                for pos in range(NSTEP + LAG + 2):
                    k += len(share(pos)) if pos < NSTEP else 0
                    k += QBLOCKS * reg_lead(pos) + reg_lead(pos - 1)
                    if pos - LAG - 1 in last_step:
                        u = last_step[pos - LAG - 1]
                        half, i = units[u]
                        k += 1
                        if half == CAUSAL:
                            wait_apart(pool, item_used, it * BODY + (LEAD + k), passed_pool)
                            b, g = it // GPB, it % GPB
                            pool.dma_start(by_group[i][bass.ds(g, 1), bass.ds(b, 1)]
                                           .rearrange("g b p t e -> (g b p) t e"),
                                           y_sb[:, u, :, :].rearrange("p (t h) d -> p t (h d)", h=HG),
                                           accum_op=ALU.add).then_inc(added, 16)
                            wait_apart(pool, added, it * (16 * QBLOCKS) + 16 * (i + 1), added_free)
                    if packed_before(pos):
                        k += 1

        @block.tensor
        def _(pe):
            ident = const["ident"]

            def slot(k):
                return small[(k - LEAD) % 3]

            def max_item(par, i, h, t, kb, k, free):
                if free is not None:
                    pe.wait_ge(item_used, free)
                diag = par == CAUSAL and kb == i
                w = P * (t + 1) if diag else QB
                lhs = qt[par][0:KMAX[par], h, i * QB + t * P:i * QB + (t + 1) * P]
                mm = nc.tensor.matmul(slot(k)[:, 0:w], lhs, kt[par][0:KMAX[par], h, kb * QB:kb * QB + w],
                                      start=True, stop=not diag)
                if diag:
                    mm = nc.tensor.matmul(slot(k)[:, w - P:w], const["ident_bf"][:, :], const["mask_max"][:, :],
                                          start=False, stop=True)
                mm.then_inc(item_made, 1)

            def turn_max(k, packs, free):
                pe.wait_ge(max_packed, packs)
                pe.wait_ge(item_used, free)
                nc.tensor.transpose(slot(k)[0:32, 0:P], packed[:, :, :].rearrange("p r a -> p (r a)"),
                                    ident[:, :]).then_inc(item_made, 1)

            pe.wait_ge(cleared, 1)
            pe.wait_ge(loaded[CAUSAL], 16 * LOADS[CAUSAL])
            k = 0
            for half, i, h, t, kb, last in lead_blocks:
                max_item(half, i, h, t, kb, k, k - 2 if k >= 3 else None)
                k += 1
                if last:
                    turn_max(k, i + 1, k - 2)
                    k += 1
            with pe.Fori(0, GROUPS) as it:
                k, e, main, turns = 0, 0, 0, 0
                for pos in range(NSTEP + LAG + 2):
                    if pos < NSTEP:
                        u, half, i, j = steps[pos]
                        if i == REG_UNIT:
                            pe.wait_ge(reg_rows_in, it * 16 + 16)
                            for two in range(2):
                                pe.wait_ge(exp_done, it * (2 * NSTEP) + (e - 1))
                                for j8 in range(8):
                                    for h in range(HG):
                                        jj = 8 * two + j8
                                        mm = nc.tensor.matmul(
                                            score[:, e % 2, 0, (j8 * HG + h) * 8:(j8 * HG + h) * 8 + 8],
                                            kt[half][0:KEXP[half], h, jj * P:(jj + 1) * P], qr[0:KEXP[half], h, 0:8],
                                            start=True, stop=True)
                                mm.then_inc(score_made, 1)
                                e += 1
                        else:
                            blocks = share(pos)
                            if j == 0:
                                pe.wait_ge(rows_in, it * (ROWS_DMA * MAIN) + ROWS_DMA * (main + 1))
                                main += 1
                            if blocks[-1][0] != half and (j == 0 or share(pos - 1)[-1][0] == half):
                                pe.wait_ge(loaded[1 - half], it * (16 * LOADS[1 - half]) + 16 * LOADS[1 - half] * (1 + half))
                            lo = P * (j - 4 * i) if half == CAUSAL and j >= 4 * i else 0
                            for two in range(2):
                                if e >= 2:
                                    pe.wait_ge(exp_done, it * (2 * NSTEP) + (e - 1))
                                for hh in range(2):
                                    h = 2 * two + hh
                                    diag = half == CAUSAL and j >= 4 * i
                                    mm = nc.tensor.matmul(score[:, e % 2, hh, lo:QB],
                                                          kt[half][0:KEXP[half], h, j * P:(j + 1) * P],
                                                          qt[half][0:KEXP[half], h, i * QB + lo:(i + 1) * QB],
                                                          start=True, stop=not diag)
                                    if diag:
                                        mm = nc.tensor.matmul(score[:, e % 2, hh, lo:lo + P],
                                                              const["ident_bf"][:, :], const["mask_exp"][:, :],
                                                              start=False, stop=True)
                                    if hh == 1:
                                        mm.then_inc(score_made, 1)
                                        e += 1
                                    for ahead, ai, ah, t, kb, _ in blocks[len(blocks) * h // HG:
                                                                          len(blocks) * (h + 1) // HG]:
                                        max_item(ahead, ai, ah, t, kb, LEAD + k, it * BODY + (LEAD + k - 2))
                                        k += 1
                        if reg_lead(pos):
                            for kb in range(QBLOCKS):
                                pe.wait_ge(item_used, it * BODY + (LEAD + k - 2))
                                for h in range(HG):
                                    mm = nc.tensor.matmul(slot(LEAD + k)[32 * h:32 * h + 32, :],
                                                          qr[0:KMAX[half], h, :],
                                                          kt[half][0:KMAX[half], h, kb * QB:(kb + 1) * QB],
                                                          start=True, stop=True)
                                mm.then_inc(item_made, 1)
                                k += 1
                        if reg_lead(pos - 1):
                            pe.wait_ge(reg_max_packed, it + 1)
                            pe.wait_ge(item_used, it * BODY + (LEAD + k - 2))
                            nc.tensor.transpose(slot(LEAD + k)[0:2, 0:P], reg_packed[:, :], ident[:, :])\
                              .then_inc(item_made, 1)
                            k += 1
                    if 0 <= pos - LAG < NSTEP:
                        s = pos - LAG
                        u, half, i, j = steps[s]
                        pe.wait_ge(exp_done, it * (2 * NSTEP) + 2 * (s + 1))
                        if j == 0 and u > 0:
                            pe.wait_ge(o_copied, it * NUNIT + u)
                        if i == REG_UNIT:
                            for jj in range(KTILES):
                                for h in range(HG):
                                    c = ((jj % 8) * HG + h) * 8
                                    mm = nc.tensor.matmul(o_ps[32 * h:32 * h + VW, 0:8], vt[half][:, jj, h, :],
                                                          prob[:, s % PRING, jj // 8, c:c + 8],
                                                          start=(jj == 0), stop=(jj == KTILES - 1))
                        else:
                            lo = P * (j - 4 * i) if half == CAUSAL and j >= 4 * i else 0
                            for h in range(HG):
                                mm = nc.tensor.matmul(o_ps[32 * h:32 * h + VW, lo:QB], vt[half][:, j, h, :],
                                                      prob[:, s % PRING, h, lo:QB],
                                                      start=(j == 0), stop=(s in last_step))
                        mm.then_inc(pv_done, 1)
                    if pos - LAG - 1 in last_step:
                        u = last_step[pos - LAG - 1]
                        pe.wait_ge(o_copied, it * NUNIT + (u + 1))
                        pe.wait_ge(item_used, it * BODY + (LEAD + k - 2))
                        if units[u][1] == REG_UNIT:
                            mm = nc.tensor.transpose(slot(LEAD + k)[0:8, 0:P], o_sb[:, u % 3, 0:8], ident[:, :])
                        else:
                            for t in range(4):
                                mm = nc.tensor.transpose(slot(LEAD + k)[:, t * P:(t + 1) * P],
                                                         o_sb[:, u % 3, t * P:(t + 1) * P], ident[:, :])
                        mm.then_inc(item_made, 1)
                        k += 1
                    if packed_before(pos):
                        turns += 1
                        turn_max(LEAD + k, it * MAIN + (LEAD_UNITS + turns), it * BODY + (LEAD + k - 2))
                        k += 1
                assert k == BODY and e == 2 * NSTEP and main == MAIN

        @block.scalar
        def _(act):
            with act.Fori(0, GROUPS) as it:
                e = 0
                for pos in range(NSTEP + LAG + 2):
                    if pos < NSTEP:
                        u, half, i, j = steps[pos]
                        lo = P * (j - 4 * i) if half == CAUSAL and j >= 4 * i else 0
                        if pos >= PRING:
                            act.wait_ge(pv_done, it * NSTEP + (pos - PRING + 1))
                        for two in range(2):
                            act.wait_ge(score_made, it * (2 * NSTEP) + (e + 1))
                            if i == REG_UNIT:
                                nc.scalar.activation(prob[:, pos % PRING, two, 0:256], score[:, e % 2, 0, 0:256],
                                                     ACT.Exp, scale=SCALE).then_inc(exp_done, 1)
                            else:
                                nc.scalar.activation(prob[:, pos % PRING, 2 * two:2 * two + 2, lo:QB],
                                                     score[:, e % 2, :, lo:QB], ACT.Exp,
                                                     scale=SCALE).then_inc(exp_done, 1)
                            e += 1
                    if pos - LAG in last_step:
                        u = last_step[pos - LAG]
                        w = 8 if units[u][1] == REG_UNIT else QB
                        act.wait_ge(pv_done, it * NSTEP + (pos - LAG + 1))
                        nc.scalar.copy(o_sb[:, u % 3, 0:w], o_ps[:, 0:w]).then_inc(o_copied, 1)

        @block.vector
        def _(dve):
            nc.vector.memset(o_ps[:, :], 0.0).then_inc(cleared, 1)
            dve.sem_inc(added_free, QBLOCKS)
            for stored in y_stored:
                dve.sem_inc(stored, 16)

            def reduce_item(k, half, i, h, t, kb, made):
                dve.wait_ge(item_made, made)
                w = P * (t + 1) if half == CAUSAL and kb == i else QB
                nc.vector.tensor_reduce(part_max[:, 4 * h + t, kb:kb + 1], small[(k - LEAD) % 3][:, 0:w], AX.X,
                                        ALU.max).then_inc(item_used, 1)

            def pack(parts_ap, minus, high, out_ap, reduced, step, packed_sem):
                dve.wait_ge(item_used, reduced)
                nc.vector.tensor_reduce(minus, parts_ap, AX.X, ALU.max, negate=True).then_inc(step_done, 1)
                dve.wait_ge(step_done, step)
                nc.vector.tensor_copy(high, minus).then_inc(step_done, 1)
                dve.wait_ge(step_done, step + 1)
                nc.vector.tensor_copy(out_ap[0], high)
                nc.vector.tensor_tensor(out_ap[1], minus, high, ALU.subtract).then_inc(packed_sem, 1)

            def turned_out(k, made, rows):
                dve.wait_ge(item_made, made)
                if rows is not None:
                    dve.wait_ge(rows_in, rows)
                nc.vector.tensor_copy(turned[:, :], small[(k - LEAD) % 3][0:32, 0:P]).then_inc(item_used, 1)

            def pack_unit(half, i, reduced, step):
                pack(part_max[:, :, 0:i + 1] if half == CAUSAL else part_max[:, :, :], minus_max[:, :], high_max[:, :],
                     (packed[:, 0, :], packed[:, 1, :]), reduced, step, max_packed)

            k = 0
            for half, i, h, t, kb, last in lead_blocks:
                reduce_item(k, half, i, h, t, kb, k + 1)
                k += 1
                if last:
                    pack_unit(half, i, k, M_STEPS * i + 1)
                    turned_out(k, k + 1, ROWS_DMA * i if i else None)
                    k += 1
            with dve.Fori(0, GROUPS) as it:
                k, c, turns = 0, 0, 0
                for pos in range(NSTEP + LAG + 2):
                    if pos < NSTEP:
                        for half, i, h, t, kb, last in share(pos):
                            reduce_item(LEAD + k, half, i, h, t, kb, it * BODY + (LEAD + k + 1))
                            k += 1
                            if last:
                                pack_unit(half, i, it * BODY + (LEAD + k), it * BODY_STEPS + (LEAD_STEPS + c + 1))
                                c += M_STEPS
                        if reg_lead(pos):
                            for kb in range(QBLOCKS):
                                dve.wait_ge(item_made, it * BODY + (LEAD + k + 1))
                                nc.vector.tensor_reduce(reg_part[:, kb:kb + 1], small[k % 3][:, :], AX.X,
                                                        ALU.max).then_inc(item_used, 1)
                                k += 1
                            pack(reg_part[:, :], reg_minus[:, :], reg_high[:, :],
                                 (reg_packed[:, 0:1], reg_packed[:, 1:2]),
                                 it * BODY + (LEAD + k), it * BODY_STEPS + (LEAD_STEPS + c + 1), reg_max_packed)
                            c += M_STEPS
                        if reg_lead(pos - 1):
                            dve.wait_ge(item_made, it * BODY + (LEAD + k + 1))
                            nc.vector.tensor_copy(reg_turned[:, :], small[k % 3][0:2, 0:P]).then_inc(item_used, 1)
                            k += 1
                    if pos - LAG - 1 in last_step:
                        u = last_step[pos - LAG - 1]
                        dve.wait_ge(item_made, it * BODY + (LEAD + k + 1))
                        reg = units[u][1] == REG_UNIT
                        rows, heads = (8, HG) if reg else (P, 4 * HG)
                        o = small[k % 3][0:rows, 0:32 * heads].rearrange("p (a e) -> p a e", e=32)
                        nc.vector.reciprocal(inv[0:rows, u % 2, 0:heads], o[:, :, D]).then_inc(step_done, 1)
                        c += 1
                        dve.wait_ge(step_done, it * BODY_STEPS + (LEAD_STEPS + c))
                        if units[u][0] == CAUSAL:
                            dve.wait_ge(added_free, it * QBLOCKS + (u + 1))
                        else:
                            dve.wait_ge(y_stored[units[u][1]], it * 16 + 16)
                        nc.vector.scalar_tensor_tensor(
                            y_sb[0:rows, u, 0:heads, :], o[:, :, 0:D],
                            const["beta"][0:rows, :] if units[u][0] == CAUSAL else 1.0,
                            inv[0:rows, u % 2, 0:heads].unsqueeze(2).broadcast_to([rows, heads, D]),
                            ALU.mult, ALU.mult).then_inc(item_used, 1)
                        k += 1
                    if packed_before(pos):
                        turned_out(LEAD + k, it * BODY + (LEAD + k + 1),
                                   it * (ROWS_DMA * MAIN) + ROWS_DMA * (LEAD_UNITS + turns))
                        turns += 1
                        k += 1
                assert k == BODY and c == BODY_STEPS


def refine_rsqrt(dve, sem, at, y, v, t):
    nc_v = dve
    nc_v.tensor_tensor(t, y, y, ALU.mult).then_inc(sem, 1)
    dve.wait_ge(sem, at + 1)
    nc_v.tensor_tensor(t, t, v, ALU.mult).then_inc(sem, 1)
    dve.wait_ge(sem, at + 2)
    nc_v.tensor_scalar(t, t, -0.5, 1.5, ALU.mult, ALU.add).then_inc(sem, 1)
    dve.wait_ge(sem, at + 3)
    nc_v.tensor_tensor(y, y, t, ALU.mult).then_inc(sem, 1)
    dve.wait_ge(sem, at + 4)


def constants(nc, sems, sb, w_attn, alpha, beta, gamma, g_info, w_qkv, w_proj, b_proj):
    c = {
        "ident": sb("ident", [P, P], F32), "ident_bf": sb("ident_bf", [P, P], BF16),
        "mask_max": sb("mask_max", [P, P], BF16), "mask_exp": sb("mask_exp", [P, P], BF16),
        "ones": sb("ones", [P, P], F32), "upto": sb("upto", [P, P], F32),
        "bias": sb("bias", [P, C], F32), "qg": sb("qg", [P, H, D], F32),
        "alpha": sb("alpha", [P, 1], F32), "beta": sb("beta", [P, 1], F32), "gamma": sb("gamma", [P, 1], F32),
        "share": sb("share", [P, KTILES], F32),
        "w_a": sb("w_a", [P, KC, 2 * C], F32), "w_f": sb("w_f", [P, KC, 3 * C], F32),
        "w_p": sb("w_p", [P, KC, C], F32),
        "head_ones": sb("head_ones", [P, P // D], F32),
        "w_v": sb("w_v", [P, KC, C + H], F32),
    }
    with ExitStack() as ctx:
        w_rows = ctx.enter_context(nc.sbuf_tensor("w_rows", [P, 4, C], F32))
        sq = ctx.enter_context(nc.sbuf_tensor("sq", [P, H, D], F32))
        n2 = ctx.enter_context(nc.sbuf_tensor("n2", [P, H], F32))
        y = ctx.enter_context(nc.sbuf_tensor("y", [P, H], F32))
        t = ctx.enter_context(nc.sbuf_tensor("t", [P, H], F32))
        turned = ctx.enter_context(nc.psum_tensor("turned_w", [P, KC, 2 * C], F32))
        w_g = ctx.enter_context(nc.sbuf_tensor("w_g", [P, KC, H, D], F32))
        w_in = sems.enter_context(nc.semaphore("const_w_in"))
        rows_in = sems.enter_context(nc.semaphore("const_rows_in"))
        filled = sems.enter_context(nc.semaphore("const_filled"))
        shaped = sems.enter_context(nc.semaphore("const_shaped"))
        w_turned = sems.enter_context(nc.semaphore("const_w_turned"))
        rooted = sems.enter_context(nc.semaphore("const_rooted"))
        done = sems.enter_context(nc.semaphore("const_steps"))
        block = ctx.enter_context(nc.Block())

        @block.sync
        def _(sp):
            sp.dma_start(w_rows[:, :, :], w_attn.rearrange("(m p) c -> p m c", p=P)).then_inc(w_in, 16)
            sp.dma_start(c["bias"][:, :], b_proj.partition_broadcast(P)).then_inc(rows_in, 16)
            sp.dma_start(c["qg"][:, :, :].rearrange("p h d -> p (h d)"), g_info[0, 0, :].partition_broadcast(P))\
              .then_inc(rows_in, 16)
            for name, ap in (("alpha", alpha), ("beta", beta), ("gamma", gamma)):
                sp.dma_start(c[name][:, :], ap.partition_broadcast(P)).then_inc(rows_in, 16)
            sp.dma_start(c["w_f"][:, :, :], w_qkv.rearrange("(k p) o -> p k o", p=P)).then_inc(rows_in, 16)
            sp.dma_start(c["w_p"][:, :, :], w_proj.rearrange("(k p) o -> p k o", p=P)).then_inc(rows_in, 16)
            sp.wait_ge(rows_in, 16 * 7)

        @block.gpsimd
        def _(pool):
            for name, value in (("ident", 0.0), ("ident_bf", 0.0), ("mask_max", 0.0), ("mask_exp", 0.0),
                                ("upto", 1.0), ("ones", 1.0), ("head_ones", 1.0)):
                nc.gpsimd.memset(c[name][:, :], value).then_inc(filled, 1)
            pool.wait_ge(filled, 7)
            for name, sign, op, fill in (("ident", 1, ALU.not_equal, 1.0), ("ident_bf", 1, ALU.not_equal, 1.0),
                                         ("mask_max", 1, ALU.is_ge, MASKED), ("mask_exp", -1, ALU.is_ge, MASKED),
                                         ("upto", -1, ALU.is_ge, 0.0)):
                nc.gpsimd.affine_select(out=c[name][:, :], in_=c[name][:, :], compare_op=op, fill=fill, base=0,
                                        pattern=[[-sign, P]], channel_multiplier=sign).then_inc(shaped, 1)
            nc.gpsimd.affine_select(out=c["head_ones"][:, :], in_=c["head_ones"][:, :], compare_op=ALU.is_ge,
                                    fill=0.0, base=0, pattern=[[-D, P // D]], channel_multiplier=1)\
              .then_inc(shaped, 1)
            pool.wait_ge(shaped, 6)
            nc.gpsimd.affine_select(out=c["head_ones"][:, :], in_=c["head_ones"][:, :], compare_op=ALU.is_ge,
                                    fill=0.0, base=D - 1, pattern=[[D, P // D]], channel_multiplier=-1)\
              .then_inc(shaped, 1)
            nc.gpsimd.iota(c["share"][:, :], pattern=[[P, KTILES]], base=1, channel_multiplier=1,
                           allow_small_or_imprecise_dtypes=True).then_inc(shaped, 1)

        @block.tensor
        def _(pe):
            pe.wait_ge(w_in, 16)
            pe.wait_ge(shaped, 1)
            for k in range(KC):
                for m in range(4):
                    mm = nc.tensor.transpose(turned[:, k, m * P:(m + 1) * P], w_rows[:, m, k * P:(k + 1) * P],
                                             c["ident"][:, :])
            mm.then_inc(w_turned, 1)

        @block.scalar
        def _(act):
            act.wait_ge(w_turned, 1)
            for k in range(KC):
                nc.scalar.copy(c["w_a"][:, k, :], turned[:, k, :])
            act.wait_ge(done, 2)
            nc.scalar.activation(y[:, :], n2[:, :], ACT.Sqrt).then_inc(rooted, 1)

        @block.vector
        def _(dve):
            dve.wait_ge(rows_in, 16 * 7)
            nc.vector.tensor_tensor(sq[:, :, :], c["qg"][:, :, :], c["qg"][:, :, :], ALU.mult).then_inc(done, 1)
            dve.wait_ge(done, 1)
            nc.vector.tensor_reduce(n2[:, :], sq[:, :, :], AX.X, ALU.add).then_inc(done, 1)
            dve.wait_ge(rooted, 1)
            nc.vector.reciprocal(y[:, :], y[:, :]).then_inc(done, 1)
            dve.wait_ge(done, 3)
            refine_rsqrt(dve, done, 3, y[:, :], n2[:, :], t[:, :])
            nc.vector.tensor_tensor(c["qg"][:, :, :], c["qg"][:, :, :],
                                    y[:, :].unsqueeze(2).broadcast_to([P, H, D]), ALU.mult).then_inc(done, 1)
            dve.wait_ge(shaped, 8)
            nc.vector.reciprocal(c["share"][:, :], c["share"][:, :]).then_inc(done, 1)
            dve.wait_ge(done, 9)
            nc.vector.tensor_scalar(c["share"][:, :], c["share"][:, :], c["gamma"][:, :], -1.0, ALU.mult,
                                    ALU.mult).then_inc(done, 1)
            for k in range(KC):
                nc.vector.tensor_tensor(w_g[:, k, :, :], c["w_f"][:, k, 0:C].rearrange("p (h d) -> p h d", d=D),
                                        c["qg"][:, :, :], ALU.mult).then_inc(done, 1)
            dve.wait_ge(done, 12)
            for k in range(KC):
                nc.vector.tensor_copy(c["w_v"][:, k, 0:C], c["w_f"][:, k, 2 * C:3 * C])
                nc.vector.tensor_reduce(c["w_v"][:, k, C:C + H], w_g[:, k, :, :], AX.X, ALU.add)
    return c


def prepare(nc, sems, x, parts, values, base_out, sims, const):
    MT = 8
    CLASS_Q = 4
    ORDER = (4, 5, 6, 7, 0, 1, 2, 3)
    VS = C + 2 * H
    with ExitStack() as ctx:
        def sb(name, shape, dt=F32):
            return ctx.enter_context(nc.sbuf_tensor(f"prep_{name}", shape, dt))

        def ps(name, shape):
            return ctx.enter_context(nc.psum_tensor(f"prep_{name}", shape, F32))

        def sem(name):
            return sems.enter_context(nc.semaphore(f"prep_{name}"))

        xs = sb("xs", [P, 2, 4, C])
        xn = sb("xn", [P, 2, 4, C])
        stats = sb("stats", [P, 4, 6])
        mv = sb("mv", [P, 4, 2])
        var = sb("var", [P, 4])
        rstd = sb("rstd", [P, 4])
        newton = sb("newton", [P, 4])
        xn_t = sb("xn_t", [P, KC, QB])
        acc = sb("acc", [P, 2, 4, C])
        base = sb("base", [P, 2, 4, C])
        whole = sb("whole", [P, 4, QB])
        rest = sb("rest", [P, 2, QB])
        split = sb("split", [P, 4, 3, QB], BF16)
        square = sb("square", [P, KC, QB])
        v_a = sb("v_a", [P, 2, GPB, 4, HG, VW])
        v_f = sb("v_f", [P, 2, GPB, 4, HG, VW])
        p_turn = ps("p_turn", [P, 4, QB])
        p_mean = ps("p_mean", [P, 2, 2, C])
        p_proj = ps("p_proj", [P, 2, QB])

        x_in = [sem(f"x_in{p}") for p in range(2)]
        x_free = sem("x_free")
        stat = sem("stat")
        std_asked = sem("std_asked")
        std_made = sem("std_made")
        xn_made = sem("xn_made")
        turn_made = sem("turn_made")
        turn_copied = sem("turn_copied")
        acc_step = sem("acc_step")
        mean_made = sem("mean_made")
        mean_used = sem("mean_used")
        base_begun = sem("base_begun")
        base_step = sem("base_step")
        base_stored = [sem(f"base_stored{p}") for p in range(2)]
        proj_made = sem("proj_made")
        whole_made = sem("whole_made")
        high_made = sem("high_made")
        rest_made = sem("rest_made")
        mid_made = sem("mid_made")
        low_made = sem("low_made")
        split_out = [sem(f"split_out{s}") for s in range(4)]
        v_made = sem("v_made")
        squared = sem("squared")
        v_copied = sem("v_copied")
        v_a_made = sem("v_a_made")
        ones_set = sem("ones_set")
        v_out = [sem(f"v_out{p}") for p in range(2)]

        x_v = x.rearrange("b (c t p) e -> (b c) p t e", p=P, t=4)
        passed_sp = sem("passed_sp")
        passed_pool = sem("passed_pool")
        passed_dve = sem("passed_dve")
        block = ctx.enter_context(nc.Block())

        @block.sync
        def _(sp):
            for p in range(2):
                sp.dma_start(xs[:, p, :, :], x_v[p]).then_inc(x_in[p], 16)
            with sp.Fori(0, B) as b:
                for c in range(4):
                    par, G = c % 2, b * 4 + c
                    wait_apart(sp, x_free, G + 1, passed_sp)
                    sp.dma_start(xs[:, par, :, :], x_v[bass.ds((G + 2) % CHUNKS, 1)]
                                 .rearrange("o p t e -> (o p) t e")).then_inc(x_in[par], 16)
                    for s, m in enumerate(ORDER):
                        wait_apart(sp, low_made, b * (4 * MT) + (MT * c + s + 1 + 2), passed_sp)
                        sp.dma_start(parts[m // 2][:, bass.ds(b * C + (m % 2) * P, P), c * QB:(c + 1) * QB]
                                     .rearrange("r p t -> p r t"), split[:, s % 4, :, :])\
                          .then_inc(split_out[s % 4], 16)
                    wait_apart(sp, base_step, b * 20 + (5 * c + 5), passed_sp)
                    sp.dma_start(base_out[bass.ds(G, 1)].rearrange("o p t e -> (o p) t e"),
                                 base[:, par, :, :]).then_inc(base_stored[par], 16)
                    wait_apart(sp, v_a_made, b * 16 + (4 * c + 4), passed_sp)
                    wait_apart(sp, v_copied, b * 16 + (4 * c + 4 + 4), passed_sp)
                    for a, v in ((0, v_a), (1, v_f)):
                        sp.dma_start(values[a][bass.ds(b * GPB, GPB), :, 4 * c * HG * VW:4 * (c + 1) * HG * VW]
                                     .rearrange("g p y -> p g y"),
                                     v[:, par, :, :, :, :].rearrange("p g t h e -> p g (t h e)"))\
                          .then_inc(v_out[par], 16)
            for p in range(2):
                sp.wait_ge(x_in[p], 16 * (CHUNKS // 2 + 1))
                sp.wait_ge(base_stored[p], 16 * (CHUNKS // 2 + 1))
                sp.wait_ge(v_out[p], 32 * (CHUNKS // 2 + 1))
            for s in range(4):
                sp.wait_ge(split_out[s], 16 * (2 * CHUNKS + 1))

        @block.tensor
        def _(pe):
            with pe.Fori(0, B) as b:
                for c in range(4):
                    par, G = c % 2, b * 4 + c
                    pe.wait_ge(xn_made, G + 1)
                    pe.wait_ge(v_copied, b * 16 + (4 * c + 2))
                    for k in range(KC):
                        for t in range(4):
                            mm = nc.tensor.transpose(p_turn[:, k, t * P:(t + 1) * P],
                                                     xn[:, par, t, k * P:(k + 1) * P], const["ident"][:, :])
                    mm.then_inc(turn_made, 1)
                    pe.wait_ge(turn_copied, b * 8 + (2 * c + 2))
                    for s, m in enumerate(ORDER):
                        w = const["w_a" if m < 4 else "w_f"]
                        pe.wait_ge(whole_made, b * (4 * MT) + (MT * c + s + 1))
                        for k in range(KC):
                            mm = nc.tensor.matmul(p_proj[:, s % 2, :], w[:, k, (m % 4) * P:(m % 4 + 1) * P],
                                                  xn_t[:, k, :], start=(k == 0), stop=(k == KC - 1))
                        mm.then_inc(proj_made, 1)
                        if s in (2, 3):
                            two = s - 2
                            pe.wait_ge(acc_step, b * 16 + (4 * c + 2 * two + 1 + 1))
                            pe.wait_ge(mean_used, b * 8 + (2 * c + two + 1))
                            for t in range(2 * two, 2 * two + 2):
                                nc.tensor.matmul(p_mean[:, two, t % 2, :], const["upto"][:, :], xn[:, par, t, :],
                                                 start=True, stop=False)
                                mm = nc.tensor.matmul(p_mean[:, two, t % 2, :], const["ones"][:, :],
                                                      acc[:, par, t, :], start=False, stop=True)
                            mm.then_inc(mean_made, 1)
                        if s >= 4:
                            t = s - 4
                            for k in range(KC):
                                nc.tensor.matmul(p_turn[:, t, 0:C + H], xn_t[:, k, t * P:(t + 1) * P],
                                                 const["w_v"][:, k, :], start=(k == 0), stop=(k == KC - 1))
                            pe.wait_ge(squared, b * (4 * KC) + KC * (c + 1))
                            for k in range(KC):
                                mm = nc.tensor.matmul(p_turn[:, t, C + H + k * P // D:C + H + (k + 1) * P // D],
                                                      square[:, k, t * P:(t + 1) * P], const["head_ones"][:, :],
                                                      start=True, stop=True)
                            mm.then_inc(v_made, 1)

        @block.scalar
        def _(act):
            act.sem_inc(whole_made, 2)
            act.sem_inc(v_copied, 4)

            def root(asked):
                act.wait_ge(std_asked, asked)
                nc.scalar.activation(rstd[:, :], var[:, :], ACT.Sqrt).then_inc(std_made, 1)

            root(1)
            with act.Fori(0, B) as b:
                for c in range(4):
                    par, G = c % 2, b * 4 + c
                    act.wait_ge(turn_made, G + 1)
                    for k in range(KC):
                        nc.scalar.copy(xn_t[:, k, :], p_turn[:, k, :]).then_inc(turn_copied, 1)
                    for s in range(MT):
                        if s == MT - 2:
                            root(G + 2)
                        act.wait_ge(proj_made, b * (4 * MT) + (MT * c + s + 1))
                        act.wait_ge(rest_made, b * (4 * MT) + (MT * c + s + 1))
                        nc.scalar.copy(whole[:, s % 4, :], p_proj[:, s % 2, :]).then_inc(whole_made, 1)
                        if s < 4:
                            if s == 0:
                                act.wait_ge(v_out[par], b * 64 + 32 * (c // 2 + 1))
                                act.wait_ge(xn_made, G + 1)
                                if c == 0:
                                    act.wait_ge(ones_set, 2)
                            nc.scalar.copy(v_a[:, par, :, s, :, 0:D],
                                           xn[:, par, s, :].rearrange("p (g h d) -> p g h d", g=GPB, d=D))\
                              .then_inc(v_a_made, 1)
                        else:
                            t = s - 4
                            act.wait_ge(v_made, b * 16 + (4 * c + t + 1 + 4))
                            nc.scalar.copy(sims[:, bass.ds(G, 1), t, :, :].rearrange("p o k h -> p (o k h)"),
                                           p_turn[:, t, C:VS])
                            nc.scalar.copy(v_f[:, par, :, t, :, 0:D],
                                           p_turn[:, t, 0:C].rearrange("p (g h d) -> p g h d", g=GPB, d=D))\
                              .then_inc(v_copied, 1)

        @block.gpsimd
        def _(pool):
            pool.sem_inc(low_made, 2)
            pool.sem_inc(v_made, 4)
            for v in (v_a, v_f):
                nc.gpsimd.memset(v[:, :, :, :, :, :], 1.0).then_inc(ones_set, 1)
            nc.gpsimd.memset(acc[:, 0, 0, :], 0.0).then_inc(acc_step, 1)
            pool.wait_ge(ones_set, 2)
            with pool.Fori(0, B) as b:
                for c in range(4):
                    par, G = c % 2, b * 4 + c
                    pool.wait_ge(xn_made, G + 1)
                    for t in range(4):
                        wait_apart(pool, acc_step, b * 16 + (4 * c + t + 1), passed_pool)
                        if t < 3 or c < 3:
                            nxt = acc[:, par, t + 1, :] if t < 3 else acc[:, 1 - par, 0, :]
                            nc.gpsimd.tensor_tensor(nxt, acc[:, par, t, :], xn[:, par, t, :], ALU.add)\
                              .then_inc(acc_step, 1)
                        else:
                            nc.gpsimd.memset(acc[:, 0, 0, :], 0.0).then_inc(acc_step, 1)
                    pool.wait_ge(base_stored[par], b * 32 + 16 * (c // 2 + 1))
                    nc.gpsimd.tensor_tensor(base[:, par, :, :], xs[:, par, :, :],
                                            const["bias"][:, :].unsqueeze(1).broadcast_to([P, 4, C]), ALU.add)\
                      .then_inc(base_begun, 1)
                    pool.wait_ge(base_begun, G + 1)
                    pool.sem_inc(x_free, 1)
                    for s in range(MT):
                        pool.wait_ge(mid_made, b * (4 * MT) + (MT * c + s + 1))
                        nc.gpsimd.tensor_tensor(split[:, s % 4, 2, :], rest[:, s % 2, :], split[:, s % 4, 1, :],
                                                ALU.subtract).then_inc(low_made, 1)

        @block.vector
        def _(dve):
            dve.sem_inc(mean_used, 2)
            dve.sem_inc(rest_made, 4)
            for p in range(2):
                dve.sem_inc(base_stored[p], 16)
                dve.sem_inc(v_out[p], 32)
            for s in range(4):
                dve.sem_inc(split_out[s], 16)
            STAT = 9

            def variance(par, x_there, base_stat):
                dve.wait_ge(x_in[par], x_there)
                for t in range(4):
                    bn = nc.vector.bn_stats(stats[:, t, :], xs[:, par, t, :])
                bn.then_inc(stat, 1)
                wait_apart(dve, stat, base_stat + 1, passed_dve)
                for t in range(4):
                    bn = nc.vector.bn_aggr(mv[:, t, :], stats[:, t, :])
                bn.then_inc(stat, 1)
                dve.wait_ge(stat, base_stat + 2)
                nc.vector.tensor_scalar(var[:, :], mv[:, :, 1], EPS, None, ALU.add).then_inc(std_asked, 1)

            def norm(par, G, base_stat):
                dve.wait_ge(std_made, G + 1)
                nc.vector.reciprocal(rstd[:, :], rstd[:, :]).then_inc(stat, 1)
                dve.wait_ge(stat, base_stat + 3)
                refine_rsqrt(dve, stat, base_stat + 3, rstd[:, :], var[:, :], newton[:, :])
                for t in range(4):
                    ts = nc.vector.tensor_scalar(xn[:, par, t, :], xs[:, par, t, :], mv[:, t, 0:1], rstd[:, t:t + 1],
                                                 ALU.subtract, ALU.mult)
                ts.then_inc(xn_made, 1)

            variance(0, 16, 0)
            norm(0, 0, 0)
            with dve.Fori(0, B) as b:
                for c in range(4):
                    par, G = c % 2, b * 4 + c
                    for s, m in enumerate(ORDER):
                        i = MT * c + s
                        dve.wait_ge(split_out[s % 4], b * 128 + 16 * (2 * c + s // 4 + 1))
                        dve.wait_ge(whole_made, b * (4 * MT) + (i + 1 + 2))
                        nc.vector.tensor_copy(split[:, s % 4, 0, :], whole[:, s % 4, :]).then_inc(high_made, 1)
                        if s < KC:
                            if s == 0:
                                dve.wait_ge(v_made, b * 16 + (4 * c + 4))
                            nc.vector.tensor_tensor(square[:, m - CLASS_Q, :], whole[:, s % 4, :],
                                                    whole[:, s % 4, :], ALU.mult).then_inc(squared, 1)
                        dve.wait_ge(high_made, b * (4 * MT) + (i + 1))
                        dve.wait_ge(low_made, b * (4 * MT) + (i + 1))
                        nc.vector.tensor_tensor(rest[:, s % 2, :], whole[:, s % 4, :], split[:, s % 4, 0, :],
                                                ALU.subtract).then_inc(rest_made, 1)
                        dve.wait_ge(rest_made, b * (4 * MT) + (i + 1 + 4))
                        nc.vector.tensor_copy(split[:, s % 4, 1, :], rest[:, s % 2, :]).then_inc(mid_made, 1)
                        if s == 2:
                            dve.wait_ge(base_begun, G + 1)
                            nc.vector.scalar_tensor_tensor(base[:, par, :, :].rearrange("p t e -> p (t e)"),
                                                           xn[:, par, :, :].rearrange("p t e -> p (t e)"),
                                                           const["alpha"][:, :],
                                                           base[:, par, :, :].rearrange("p t e -> p (t e)"),
                                                           ALU.mult, ALU.add).then_inc(base_step, 1)
                        if s in (3, 5):
                            two = (s - 3) // 2
                            dve.wait_ge(base_step, b * 20 + (5 * c + 1))
                            dve.wait_ge(mean_made, b * 8 + (2 * c + two + 1))
                            for t in range(2 * two, 2 * two + 2):
                                nc.vector.scalar_tensor_tensor(
                                    base[:, par, t, :], p_mean[:, two, t % 2, :],
                                    const["share"][:, 4 * c + t:4 * c + t + 1],
                                    base[:, par, t, :], ALU.mult, ALU.add).then_inc(base_step, 1)
                            dve.wait_ge(base_step, b * 20 + (5 * c + 2 * two + 3))
                            dve.sem_inc(mean_used, 1)
                        if s == 4:
                            variance(1 - par, b * 32 + 16 * ((c + 1) // 2 + 1), b * (4 * 7) + 7 * (c + 1))
                        if s == 5:
                            norm(1 - par, G + 1, b * (4 * 7) + 7 * (c + 1))


def classify(nc, sems, sims, masks, reg_rows, ops, parts, values, const):
    NT = B * KTILES
    dots, norms = [sims[:, :, :, k, :].rearrange("p c t h -> p (c t) h") for k in range(2)]
    with ExitStack() as ctx:
        def sb(name, shape, dt=F32):
            return ctx.enter_context(nc.sbuf_tensor(f"class_{name}", shape, dt))

        root = sb("root", [P, NT, H])
        newton = sb("newton", [P, NT, H])
        sim = sb("sim", [P, NT])
        edge = sb("edge", [P, 2, NT])
        ends = sb("ends", [P, 2])
        both = sb("both", [P, 2])
        width = sb("width", [P, 1])
        pos = sb("pos", [P, NT])
        rows = sb("rows", [P, 4, NT])
        rows_t = sb("rows_t", [P, 2, P], BF16)
        reg = sb("reg", [2, P], BF16)
        p_rows = ctx.enter_context(nc.psum_tensor("p_rows", [P, 2, P], F32))
        rooted = sems.enter_context(nc.semaphore("class_rooted"))
        step = sems.enter_context(nc.semaphore("class_step"))
        ends_made = sems.enter_context(nc.semaphore("class_ends_made"))
        ends_shared = sems.enter_context(nc.semaphore("class_ends_shared"))
        rows_made = sems.enter_context(nc.semaphore("class_rows_made"))
        rows_turned = sems.enter_context(nc.semaphore("class_rows_turned"))
        rows_ready = sems.enter_context(nc.semaphore("class_rows_ready"))
        stored = sems.enter_context(nc.semaphore("class_stored"))
        block = ctx.enter_context(nc.Block())

        @block.scalar
        def _(act):
            nc.scalar.activation(root[:, :, :], norms, ACT.Sqrt).then_inc(rooted, 1)

        @block.gpsimd
        def _(pool):
            for kt in ops["kt"]:
                nc.gpsimd.memset(kt[SPLIT_ROWS:SPLIT_ROWS + 4, :, :], 1.0).then_inc(ops["ones_set"], 1)
            pool.wait_ge(ops["ones_set"], 2)
            pool.wait_ge(ends_made, 1)
            nc.gpsimd.partition_all_reduce(both[:, :], ends[:, :], P, bass.bass_isa.ReduceOp.max)\
              .then_inc(ends_shared, 1)

        @block.tensor
        def _(pe):
            pe.wait_ge(rows_made, 1)
            for a in range(2):
                mm = nc.tensor.transpose(p_rows[:, a, :], rows[:, 2 * a:2 * a + 2, :].rearrange("p k t -> p (k t)"),
                                         const["ident"][:, :])
            mm.then_inc(rows_turned, 1)

        @block.sync
        def _(sp):
            load(sp, ops, 0, CAUSAL, parts, values, masks, reg_rows)
            sp.wait_ge(rows_ready, 1)
            for k in range(4):
                sp.dma_start(masks[k].rearrange("b (t x) -> (b t) x", x=P),
                             rows_t[64 * (k % 2):64 * (k % 2) + 64, k // 2, :]).then_inc(stored, 16)
            sp.dma_start(reg_rows, reg[:, :]).then_inc(stored, 16)
            sp.wait_ge(stored, 16 * 5)
            sp.wait_ge(ops["ones_set"], 2)
            sp.wait_ge(ops["loaded"][CAUSAL], 16 * LOADS[CAUSAL])

        @block.vector
        def _(dve):
            count = [0]

            def link(ins):
                ins.then_inc(step, 1)
                count[0] += 1
                dve.wait_ge(step, count[0])

            link(nc.vector.memset(reg[:, :], 0.0))
            link(nc.vector.memset(reg[0:1, :], MASKED))
            dve.wait_ge(rooted, 1)
            link(nc.vector.reciprocal(root[:, :, :], root[:, :, :]))
            refine_rsqrt(dve, step, count[0], root[:, :, :], norms, newton[:, :, :])
            count[0] += 4
            link(nc.vector.tensor_tensor(root[:, :, :], root[:, :, :], dots, ALU.mult))
            link(nc.vector.tensor_reduce(sim[:, :], root[:, :, :], AX.X, ALU.add))
            link(nc.vector.tensor_scalar(sim[:, :], sim[:, :], 1.0 / H, None, ALU.mult))
            nc.vector.tensor_copy(edge[:, 0, :], sim[:, :])
            link(nc.vector.tensor_scalar(edge[:, 1, :], sim[:, :], -1.0, None, ALU.mult))
            link(nc.vector.memset(edge[0:REG, :, 0:NT:KTILES], -3e38))
            nc.vector.tensor_reduce(ends[:, :], edge[:, :, :], AX.X, ALU.max).then_inc(ends_made, 1)
            dve.wait_ge(ends_shared, 1)
            link(nc.vector.tensor_tensor(width[:, :], both[:, 0:1], both[:, 1:2], ALU.add))
            link(nc.vector.reciprocal(width[:, :], width[:, :]))
            link(nc.vector.tensor_scalar(sim[:, :], sim[:, :], both[:, 1:2], width[:, :], ALU.add, ALU.mult))
            link(nc.vector.tensor_scalar(pos[:, :], sim[:, :], 0.9, None, ALU.is_gt))
            nc.vector.tensor_copy(rows[:, 0, :], pos[:, :])
            link(nc.vector.tensor_scalar(rows[:, 1, :], pos[:, :], -1.0, 1.0, ALU.mult, ALU.add))
            link(nc.vector.memset(rows[0:REG, 0:2, 0:NT:KTILES], 0.0))
            link(nc.vector.memset(pos[0:REG, 0:NT:KTILES], 1.0))
            nc.vector.tensor_scalar(rows[:, 2, :], pos[:, :], -MASKED, MASKED, ALU.mult, ALU.add)
            nc.vector.tensor_scalar(rows[:, 3, :], pos[:, :], MASKED, None, ALU.mult).then_inc(rows_made, 1)
            dve.wait_ge(rows_turned, 1)
            nc.vector.tensor_copy(rows_t[:, :, :], p_rows[:, :, :]).then_inc(rows_ready, 1)


def finish(nc, sems, base_in, y_f, y_reg, out, const):
    CAME = 16 * (1 + GPB)
    BUFS = QBLOCKS
    AHEAD = BUFS - 1
    with ExitStack() as ctx:
        def sb(name, shape):
            return ctx.enter_context(nc.sbuf_tensor(f"fin_{name}", shape, F32))

        def sem(name):
            return sems.enter_context(nc.semaphore(f"fin_{name}"))

        yf = sb("yf", [P, BUFS, 4, GPB, HG * D])
        yr = sb("yr", [8, B, GPB, HG * D])
        base = sb("base", [P, BUFS, 4, C])
        yt = sb("yt", [P, 2, KC, QB])
        res = sb("res", [P, BUFS, 4, C])
        p_turn = ctx.enter_context(nc.psum_tensor("fin_turn", [P, 2, KC, QB], F32))
        p_out = ctx.enter_context(nc.psum_tensor("fin_out", [P, 2, 2, C], F32))
        came = [sem(f"came{p}") for p in range(BUFS)]
        reg_came = sem("reg_came")
        reg_step = sem("reg_step")
        turned = sem("turned")
        copied = sem("copied")
        made = sem("made")
        summed = sem("summed")
        stored = [sem(f"stored{p}") for p in range(BUFS)]
        out_v = out.rearrange("b (c t p) e -> (b c) p t e", p=P, t=4)
        passed_sp = sem("passed_sp")
        block = ctx.enter_context(nc.Block())

        @block.sync
        def _(sp):
            def load(n, par, b, c):
                for g in range(GPB):
                    sp.dma_start(yf[:, par, :, g, :], y_f[bass.ds(b * GPB + g, 1), c]
                                 .rearrange("o p (t e) -> (o p) t e", t=4)).then_inc(came[par], 16)
                sp.dma_start(base[:, par, :, :], base_in[bass.ds(n, 1)].rearrange("o p t e -> (o p) t e"))\
                  .then_inc(came[par], 16)

            sp.dma_start(yr[:, :, :, :].rearrange("r b g x -> r (b g) x"), y_reg.rearrange("n r x -> r n x"))\
              .then_inc(reg_came, 16)
            for c in range(AHEAD):
                load(c, c, 0, c)

            def batch(b, loads):
                for c in range(4):
                    G = b * 4 + c
                    if c in loads:
                        wait_apart(sp, summed, b * 8 + (2 * c + 2), passed_sp)
                        load((G + AHEAD) % CHUNKS, (c + AHEAD) % BUFS, b if c == 0 else (b + 1) % B,
                             (c + AHEAD) % BUFS)
                    wait_apart(sp, summed, b * 8 + (2 * c + 2 + 2), passed_sp)
                    sp.dma_start(out_v[bass.ds(G, 1)].rearrange("o p t e -> (o p) t e"), res[:, c, :, :])\
                      .then_inc(stored[c], 16)

            with sp.Fori(0, B - 1) as b:
                batch(b, range(4))
            batch(B - 1, (0, 1))
            for p in range(BUFS):
                sp.wait_ge(came[p], CAME * (B + (p == 0)))
                sp.wait_ge(stored[p], 16 * (B + 1))

        @block.tensor
        def _(pe):
            with pe.Fori(0, B) as b:
                for c in range(4):
                    pe.wait_ge(came[c], b * CAME + CAME)
                    if c == 0:
                        pe.wait_ge(reg_step, b * 2 + 2)
                    for k in range(KC):
                        for t in range(4):
                            mm = nc.tensor.transpose(p_turn[:, c % 2, k, t * P:(t + 1) * P],
                                                     yf[:, c, t, 2 * k:2 * k + 2, :].rearrange("p g e -> p (g e)"),
                                                     const["ident"][:, :])
                        mm.then_inc(turned, 1)
                    pe.wait_ge(copied, b * 8 + (2 * c + 2))
                    for two in range(2):
                        pe.wait_ge(summed, b * 8 + (2 * c + two + 1))
                        for t in range(2 * two, 2 * two + 2):
                            for k in range(KC):
                                mm = nc.tensor.matmul(p_out[:, two, t % 2, :], yt[:, c % 2, k, t * P:(t + 1) * P],
                                                      const["w_p"][:, k, :], start=(k == 0), stop=(k == KC - 1))
                        mm.then_inc(made, 1)

        @block.scalar
        def _(act):
            with act.Fori(0, B) as b:
                for c in range(4):
                    for k in range(KC):
                        act.wait_ge(turned, b * 8 + (2 * c + k + 1))
                        nc.scalar.copy(yt[:, c % 2, k, :], p_turn[:, c % 2, k, :]).then_inc(copied, 1)

        @block.vector
        def _(dve):
            dve.sem_inc(summed, 2)
            for p in range(BUFS):
                dve.sem_inc(stored[p], 16)
            dve.wait_ge(reg_came, 16)

            def average(b, slot_b):
                dve.wait_ge(came[0], b * CAME + CAME)
                nc.vector.tensor_tensor(yf[0:REG, 0, 0, :, :], yf[0:REG, 0, 0, :, :],
                                        yr[0:REG, bass.ds(slot_b, 1), :, :].rearrange("r o g x -> r (o g) x"),
                                        ALU.add).then_inc(reg_step, 1)
                dve.wait_ge(reg_step, b * 2 + 1)
                nc.vector.tensor_scalar(yf[0:REG, 0, 0, :, :], yf[0:REG, 0, 0, :, :], 0.5, None,
                                        ALU.mult).then_inc(reg_step, 1)

            average(0, 0)
            with dve.Fori(0, B) as b:
                for c in range(4):
                    if c == 3:
                        average(b + 1, (b + 1) % B)
                    dve.wait_ge(stored[c], b * 16 + 16)
                    for two in range(2):
                        dve.wait_ge(made, b * 8 + (2 * c + two + 1))
                        nc.vector.tensor_tensor(res[:, c, 2 * two:2 * two + 2, :], p_out[:, two, :, :],
                                                base[:, c, 2 * two:2 * two + 2, :], ALU.add).then_inc(summed, 1)


def build(nc, x, w_attn, alpha, beta, gamma, g_info, w_qkv, w_proj, b_proj, out):
    def dram(name, shape, dt=F32):
        return nc.dram_tensor(name, shape, dt, kind="Internal").ap()

    parts = dram("parts", (4, 3, B * C, T), BF16)
    values = dram("values", (2, GROUPS, P, KTILES * HG * VW))
    base = dram("base", (CHUNKS, P, 4, C))
    masks = dram("masks", (4, B, T), BF16)
    reg_rows = dram("reg_rows", (2, P), BF16)
    y_f = dram("y_f", (GROUPS, QBLOCKS, P, 4 * HG * D))
    y_reg = dram("y_reg", (GROUPS, 8, HG * D))
    with ExitStack() as ctx:
        def sb(name, shape, dt):
            return ctx.enter_context(nc.sbuf_tensor(name, shape, dt))

        const = constants(nc, ctx, sb, w_attn, alpha, beta, gamma, g_info, w_qkv, w_proj, b_proj)
        ops = operands(nc, ctx)
        with ExitStack() as early:
            sims = early.enter_context(nc.sbuf_tensor("sims", [P, CHUNKS, 4, 2, H], F32))
            prepare(nc, ctx, x, parts, values, base, sims, const)
            classify(nc, ctx, sims, masks, reg_rows, ops, parts, values, const)
        attend(nc, ctx, ops, parts, values, masks, reg_rows, base, y_f, y_reg, const)
        finish(nc, ctx, base, y_f, y_reg, out, const)


_INS = ["L0_attn_x", "L0_attn_W_attn", "L0_attn_alpha", "L0_attn_beta", "L0_attn_gamma", "L0_ffn_g_info",
        "L0_ffn_W_qkv", "L0_ffn_W_proj", "L0_ffn_b_proj"]


def kernel(**inputs):
    import concourse.bacc as _bacc
    from concourse.bass_utils import run_bass_kernel_spmd as _run

    nc = _bacc.Bacc("TRN2", target_bir_lowering=False, num_devices=1)
    arrays, args = {}, []
    for name in _INS:
        a = np.ascontiguousarray(inputs[name])
        arrays[f"in_{name}"] = a
        args.append(nc.dram_tensor(f"in_{name}", a.shape, mybir.dt.from_np(a.dtype), kind="ExternalInput").ap())
    out = nc.dram_tensor("out_0", (B, T, C), F32, kind="ExternalOutput").ap()
    build(nc, *args, out)
    return _run(nc, [arrays], core_ids=[0]).results[0]["out_0"]
```
